# Optimizing a Trainium2 kernel written in Bass

```python
import numpy as np
import jax
import jax.numpy as jnp

def _softmax(x, axis=-1):
    return jax.nn.softmax(x, axis=axis)

def _gelu(x):
    return jax.nn.gelu(x, approximate=True)

def _silu(x):
    return jax.nn.silu(x)

def _sigmoid(x):
    return jax.nn.sigmoid(x)

def _layernorm(x, axis=-1, eps=1e-05):
    m = jnp.mean(x, axis=axis, keepdims=True)
    v = jnp.var(x, axis=axis, keepdims=True)
    return (x - m) / jnp.sqrt(v + eps)

def _scatter_add(tgt, idx, src, axis=0):
    return tgt.at[idx].add(src)

def _segment_sum(src, seg, n):
    return jax.ops.segment_sum(src, seg, n)
kernel_name = 'mk_flamingo_gated_d1_seqx_r4_7c36c7'

def setup_inputs(seed: int=0):
    np.random.seed(seed)
    _w = jnp.asarray

    def _rec_inputs():
        import jax
        import jax.numpy as jnp
        _rk = jax.random.key(seed)
        x = 7.22e-05 + 1 * jax.random.normal(jax.random.fold_in(_rk, 1), (8, 256, 512), jnp.float32)
        _lenS = 256 - jax.random.randint(jax.random.fold_in(_rk, 7), (8,), 0, max(1, 256 // 4) + 1, jnp.int32)
        _lenS2 = 256 - jax.random.randint(jax.random.fold_in(_rk, 8), (8,), 0, max(1, 256 // 4) + 1, jnp.int32)
        _ctx_2048P = jax.random.normal(jax.random.fold_in(_rk, 11), (8, 16, 512), jnp.float32)
        _ctx_2048c = jax.random.dirichlet(jax.random.fold_in(_rk, 511), 0.3 * jnp.ones((16,), jnp.float32), (8, 256))
        _ctx_2048t = jnp.einsum('bsk,bkd->bsd', _ctx_2048c, _ctx_2048P)
        _ctx_2048t = _ctx_2048t * jax.lax.rsqrt(jnp.mean(jnp.square(_ctx_2048t)) + 1e-12) * 0.953939
        ctx_2048 = 4.13588e-05 + 0.999923 * (_ctx_2048t + 0.3 * jax.random.normal(jax.random.fold_in(_rk, 611), (8, 256, 512), jnp.float32))
        _g = jax.random.normal(jax.random.fold_in(_rk, 9001), (2, 1), jnp.float32)
        _g = jnp.sign(_g) * jnp.maximum(jnp.abs(_g), 1.0) + (_g == 0) * 1.0
        g_xattn = _g[0]
        g_ffn = _g[1]
        return (x, ctx_2048, g_xattn, g_ffn)
    x, ctx_2048, g_xattn, g_ffn = _rec_inputs()

    def _L0_xattn_setup():
        import jax, jax.numpy as jnp
        import numpy as np
        B, S, DIM, HD = (4, 256, 512, 128)
        H = DIM // HD
        GN_EPS = 0.001

        def _decay_masks(n_heads, seq_len):
            gam = 1.0 - 2.0 ** (-5.0 - jnp.arange(n_heads, dtype=jnp.float32))
            idx = jnp.arange(seq_len, dtype=jnp.float32)
            expo = idx[None, :] - idx[:, None]
            D = jnp.where(expo[None, :, :] <= 0, gam[:, None, None] ** expo[None, :, :], 0.0)
            return D / jnp.sqrt(D.sum(axis=-1))[:, None, :]
        key = jax.random.key(seed)
        ks = jax.random.split(key, 8)
        x = jax.random.normal(ks[0], (B, S, DIM), dtype=jnp.float32)
        k = jax.random.normal(ks[1], (B, S, DIM), dtype=jnp.float32)
        v = jax.random.normal(ks[2], (B, S, DIM), dtype=jnp.float32)
        Wh = jax.random.normal(ks[3], (H, HD, HD), dtype=jnp.float32) / np.sqrt(HD)
        wg_w = jax.random.normal(ks[4], (DIM, DIM), dtype=jnp.float32) / np.sqrt(DIM)
        wo_w = jax.random.normal(ks[5], (DIM, DIM), dtype=jnp.float32) / np.sqrt(DIM)
        gn_gamma = jnp.ones((DIM,), dtype=jnp.float32)
        gn_beta = jnp.zeros((DIM,), dtype=jnp.float32)
        return {'x': x, 'k': k, 'v': v, 'Wh': Wh, 'wg_w': wg_w, 'wo_w': wo_w, 'gn_gamma': gn_gamma, 'gn_beta': gn_beta}
    _L0_xattn_all = _L0_xattn_setup()
    _L0_xattn_in = {k: v for k, v in _L0_xattn_all.items() if k in ('Wh', 'wg_w', 'wo_w', 'gn_gamma', 'gn_beta')}
    del _L0_xattn_all

    def _L0_ffn_setup():
        import jax, jax.numpy as jnp
        import numpy as np
        B, S, DIM = (2, 512, 512)
        E, K = (8, 2)
        H = DIM * 4 // 3
        key = jax.random.key(seed)
        ks = jax.random.split(key, 8)
        s = 0.02
        x = jax.random.normal(ks[0], (B, S, DIM), dtype=jnp.float32)
        sw1 = jax.random.normal(ks[1], (H, DIM), dtype=jnp.float32) * s
        sw2 = jax.random.normal(ks[2], (DIM, H), dtype=jnp.float32) * s
        sw3 = jax.random.normal(ks[3], (H, DIM), dtype=jnp.float32) * s
        ew1 = jax.random.normal(ks[4], (E, H, DIM), dtype=jnp.float32) * s
        ew2 = jax.random.normal(ks[5], (E, DIM, H), dtype=jnp.float32) * s
        ew3 = jax.random.normal(ks[6], (E, H, DIM), dtype=jnp.float32) * s
        wr = jax.random.normal(ks[7], (E, DIM), dtype=jnp.float32) * s
        return {'x': x, 'sw1': sw1, 'sw2': sw2, 'sw3': sw3, 'ew1': ew1, 'ew2': ew2, 'ew3': ew3, 'wr': wr}
    _L0_ffn_all = _L0_ffn_setup()
    _L0_ffn_in = {k: v for k, v in _L0_ffn_all.items() if k in ('sw1', 'sw2', 'sw3', 'ew1', 'ew2', 'ew3', 'wr')}
    del _L0_ffn_all
    return {'x': x, 'ctx_2048': ctx_2048, 'g_xattn': g_xattn, 'g_ffn': g_ffn, 'L0_xattn_Wh': _L0_xattn_in['Wh'], 'L0_xattn_wg_w': _L0_xattn_in['wg_w'], 'L0_xattn_wo_w': _L0_xattn_in['wo_w'], 'L0_xattn_gn_gamma': _L0_xattn_in['gn_gamma'], 'L0_xattn_gn_beta': _L0_xattn_in['gn_beta'], 'L0_ffn_sw1': _L0_ffn_in['sw1'], 'L0_ffn_sw2': _L0_ffn_in['sw2'], 'L0_ffn_sw3': _L0_ffn_in['sw3'], 'L0_ffn_ew1': _L0_ffn_in['ew1'], 'L0_ffn_ew2': _L0_ffn_in['ew2'], 'L0_ffn_ew3': _L0_ffn_in['ew3'], 'L0_ffn_wr': _L0_ffn_in['wr']}

def reference(x, ctx_2048, g_xattn, g_ffn, L0_xattn_Wh, L0_xattn_wg_w, L0_xattn_wo_w, L0_xattn_gn_gamma, L0_xattn_gn_beta, L0_ffn_sw1, L0_ffn_sw2, L0_ffn_sw3, L0_ffn_ew1, L0_ffn_ew2, L0_ffn_ew3, L0_ffn_wr):
    import jax
    import jax.numpy as jnp

    def _L0_xattn_ref(x, k, v, Wh, wg_w, wo_w, gn_gamma, gn_beta):
        import jax, jax.numpy as jnp
        import numpy as np
        B, S, DIM, HD = (4, 256, 512, 128)
        H = DIM // HD
        GN_EPS = 0.001

        def _decay_masks(n_heads, seq_len):
            gam = 1.0 - 2.0 ** (-5.0 - jnp.arange(n_heads, dtype=jnp.float32))
            idx = jnp.arange(seq_len, dtype=jnp.float32)
            expo = idx[None, :] - idx[:, None]
            D = jnp.where(expo[None, :, :] <= 0, gam[:, None, None] ** expo[None, :, :], 0.0)
            return D / jnp.sqrt(D.sum(axis=-1))[:, None, :]
        b, s, dim = x.shape
        h, hd, _ = Wh.shape
        xh = x.reshape(b, s, h, hd)
        kh = k.reshape(b, s, h, hd)
        vh = v.reshape(b, s, h, hd)
        Q = jnp.einsum('bshd,hde->bshe', xh, Wh)
        K = jnp.einsum('bshd,hde->bshe', kh, Wh)
        V = jnp.einsum('bshd,hde->bshe', vh, Wh)
        scores = jnp.einsum('bshe,bthe->bhst', Q, K) / jnp.sqrt(jnp.float32(hd))
        Dn = _decay_masks(h, s)
        masked = scores * Dn[None, :, :, :]
        A = jnp.maximum(jnp.abs(masked.sum(axis=0)), 1.0)
        O = jnp.einsum('hst,bthe->bshe', A, V).reshape(b, s, dim)
        mu = O.mean(axis=-1, keepdims=True)
        var = O.var(axis=-1, keepdims=True)
        Y = (O - mu) / jnp.sqrt(var + GN_EPS) * gn_gamma + gn_beta
        W = jax.nn.relu(x @ wg_w)
        return W * Y @ wo_w

    def _L0_ffn_ref(x, sw1, sw2, sw3, ew1, ew2, ew3, wr):
        import jax, jax.numpy as jnp
        import numpy as np
        B, S, DIM = (2, 512, 512)
        E, K = (8, 2)
        H = DIM * 4 // 3
        shared = jax.nn.silu(x @ sw1.T) * (x @ sw3.T) @ sw2.T
        logits = x @ wr.T
        probs = jax.nn.softmax(logits, axis=-1)
        top_p, top_i = jax.lax.top_k(probs, K)
        top_p = top_p / jnp.sum(top_p, axis=-1, keepdims=True)
        gates = jnp.sum(jax.nn.one_hot(top_i, E, dtype=x.dtype) * top_p[..., None], axis=-2)
        u = jnp.einsum('bsd,ehd->bseh', x, ew1)
        v = jnp.einsum('bsd,ehd->bseh', x, ew3)
        h = jax.nn.silu(u) * v
        eo = jnp.einsum('bseh,edh->bsed', h, ew2)
        return shared + jnp.einsum('bsed,bse->bsd', eo, gates)
    x = x + jnp.tanh(g_xattn[0]) * _L0_xattn_ref(_layernorm(x, axis=-1), ctx_2048, ctx_2048, L0_xattn_Wh, L0_xattn_wg_w, L0_xattn_wo_w, L0_xattn_gn_gamma, L0_xattn_gn_beta)
    x = x + jnp.tanh(g_ffn[0]) * _L0_ffn_ref(_layernorm(x, axis=-1), L0_ffn_sw1, L0_ffn_sw2, L0_ffn_sw3, L0_ffn_ew1, L0_ffn_ew2, L0_ffn_ew3, L0_ffn_wr)
    return x

_drawn_inputs = setup_inputs


def setup_inputs(seed=0):
    import zlib

    import numpy as np

    out = dict(_drawn_inputs(seed))
    spreads = {'L0_xattn_gn_gamma': (1.0, 0.2), 'L0_xattn_gn_beta': (0.0, 0.1)}
    factors = {}
    for name, (base, spread) in spreads.items():
        noise = np.random.default_rng([zlib.crc32(name.encode()), seed]).standard_normal(out[name].shape)
        drawn = base * np.exp(spread * noise) if base else spread * noise
        out[name] = jnp.asarray(drawn.astype(out[name].dtype))
    for name, factor in factors.items():
        out[name] = (out[name] * factor).astype(out[name].dtype)
    return out
```

```python
from contextlib import ExitStack

import numpy as np

import concourse.bass as bass
from concourse import mybir

F32 = mybir.dt.float32
F32R = mybir.dt.float32r
I32 = mybir.dt.int32
ALU = mybir.AluOpType
ACT = mybir.ActivationFunctionType
X = mybir.AxisListType.X

P = 128
B, S, D = 8, 256, 512
HEADS, HD = 4, 128
N = B * S
TILES = N // P
KD = D // P
E = 8
HID = D * 4 // 3
HC = HID // P
HT = HID - HC * P
FIRST = 10
LAST = TILES - FIRST
ROUTED = (2 * N - E) // P + E
STEPS = FIRST + ROUTED + LAST
THR = N // P
EPS1, EPS_GN = 1e-5, 1e-3


def attention(nc, io, keep, banks):
    ctx = ExitStack()
    with ctx:
        def sb(name, shape, dt=F32):
            return ctx.enter_context(nc.sbuf_tensor(name, shape, dt))

        def sem(name):
            return ctx.enter_context(nc.semaphore(name))

        x = keep["x"]
        ident = keep["ident"]
        xn = sb("xn", [P, 2, D])
        xnT = sb("xnT", [P, KD, N])
        ctxT = sb("ctxT", [P, 2, N])
        wh = sb("wh", [P, HEADS, HD])
        wg = sb("wg", [P, KD, D])
        wo = sb("wo", [P, KD, D])
        wr = sb("wr", [P, KD, E])
        mask = sb("mask", [P, HEADS, 2, S])
        gamma = sb("gamma", [P, D])
        beta = sb("beta", [P, D])
        QT = sb("QT", [P, 2, N])
        KT = sb("KT", [P, 2, N])
        V = sb("V", [P, 2, 2, B, HD])
        AT = sb("AT", [P, 2, 2, S])
        masked = sb("masked", [P, S])
        O = sb("O", [P, 2, B, HEADS, HD])
        stats = sb("stats", [P, 3 * TILES, 6])
        mv = sb("mv", [P, 3 * TILES, 2])
        var_eps = sb("var_eps", [P, 3 * TILES])
        rstd = sb("rstd", [P, 3 * TILES])
        neg_half = sb("neg_half", [P, 1])
        Y = QT[:, 0, 0:D]
        Z = QT[:, 0, D:3 * D].rearrange("p (a n) -> p a n", a=2)
        ZT = QT[:, 1, 0:2 * D].rearrange("p (a k n) -> p a k n", a=2, k=KD)
        xn2T = QT[:, 1, 2 * D:4 * D].rearrange("p (a k n) -> p a k n", a=2, k=KD)

        P0, P1, P2, P3, S0, S1, T0, T1 = banks
        ring = [P0, P1, P2, P3]

        x_in = [sem(f"x_in{q}") for q in range(4)]
        ctx_in = [sem(f"ctx_in{h}") for h in range(HEADS)]
        wh_in, mask_in, wg_in, wo_in = sem("wh_in"), sem("mask_in"), sem("wg_in"), sem("wo_in")
        gb_in, wr_in, gate_in, ident_in = sem("gb_in"), sem("wr_in"), sem("gate_in"), sem("ident_in")
        pad_zero, pads_set = sem("pad_zero"), sem("pads_set")
        dve_step = sem("dve_step")
        half_set, mv_ready, var_ready, rstd_ready = (sem("half_set"), sem("mv_ready"), sem("var_ready"),
                                                    sem("rstd_ready"))
        xn_ready, xn_turned, xnT_ready = sem("xn_ready"), sem("xn_turned"), sem("xnT_ready")
        fill_done, act_evac, dve_evac = sem("fill_done"), sem("act_evac"), sem("dve_evac")
        s_done, at_ready = sem("s_done"), sem("at_ready")
        gates_ready = sem("gates_ready")
        w_done, z_ready, z_turned, zT_ready = sem("w_done"), sem("z_ready"), sem("z_turned"), sem("zT_ready")
        wo_done, xn2_ready, xn2_turned, xn2T_ready = (sem("wo_done"), sem("xn2_ready"),
                                                      sem("xn2_turned"), sem("xn2T_ready"))
        xn2_out = [sem(f"xn2_out{q}") for q in range(2)]
        logits_done = sem("logits_done")
        block = ctx.enter_context(nc.Block())

        zeros = O[:, 1, B - 1, :, :].rearrange("p h e -> p (h e)")

        def qkv(h):
            return [(kind, h, c) for kind in "QKV" for c in range(4)]

        plan = qkv(0)
        for h in range(HEADS):
            plan.append(("S", h, 0))
            if h + 1 < HEADS:
                plan += qkv(h + 1)
            plan += [("O", h, c) for c in range(4)]
        fill_of, r = {}, 0
        for item in plan:
            if item[0] != "S":
                fill_of[item] = r
                r += 1

        slot_order = [(i, EPS1) for i in range(TILES)] + [(TILES, EPS_GN), (TILES + 1, EPS_GN)]
        for t in range(TILES + 2):
            if t + 2 < TILES:
                slot_order.append((TILES + t + 2, EPS_GN))
            if t >= 2:
                slot_order.append((2 * TILES + t - 2, EPS1))
        turn_of = {slot: n for n, (slot, _) in enumerate(slot_order)}

        def destination(kind, h, c):
            if kind == "Q":
                return QT[:, h % 2, c * 512:(c + 1) * 512]
            if kind == "K":
                return KT[:, h % 2, c * 512:(c + 1) * 512]
            if kind == "V":
                return V[:, h % 2, :, 2 * c:2 * c + 2, :].rearrange("p t b e -> p b t e")
            return O[:, c // 2, 4 * (c % 2):4 * (c % 2) + 4, h, :]

        def source(kind, bank):
            if kind == "V":
                return bank[:, :].rearrange("p (b t e) -> p b t e", b=2, t=2)
            if kind == "O":
                return bank[:, :].rearrange("p (b e) -> p b e", b=4)
            return bank[:, :]

        @block.sync
        def _(sp):
            sp.dma_start(ident[:, :], io["ident"]).then_inc(ident_in, 16)
            for q in range(4):
                sp.dma_start(x[:, 4 * q:4 * q + 4, :],
                             io["x"][512 * q:512 * q + 512, :].rearrange("(t p) d -> p t d", p=P)
                             ).then_inc(x_in[q], 16)
            sp.dma_start(wh[:, :, :], io["wh"].rearrange("h d e -> d h e")).then_inc(wh_in, 16)
            for h in range(2):
                sp.dma_start(ctxT[:, h, :], io["ctxT"][h * P:(h + 1) * P, :]).then_inc(ctx_in[h], 16)
            sp.dma_start(mask[:, :, :, :], io["mask"]).then_inc(mask_in, 16)
            sp.dma_start(wg[:, :, :], io["wg"].rearrange("(k p) n -> p k n", p=P)).then_inc(wg_in, 16)
            sp.dma_start(wo[:, :, :], io["wo"].rearrange("(k p) n -> p k n", p=P)).then_inc(wo_in, 16)
            sp.dma_start(wr[:, :, :], io["wrT"].rearrange("(k p) n -> p k n", p=P)).then_inc(wr_in, 16)
            sp.dma_start(gamma[:, :], io["gamma"].to_broadcast([P, D])).then_inc(gb_in, 16)
            sp.dma_start(beta[:, :], io["beta"].to_broadcast([P, D])).then_inc(gb_in, 16)
            sp.wait_ge(pad_zero, 1)
            for q in range(ROUTED // 3):
                sp.dma_start(io["slots"][3 * P * q:3 * P * (q + 1), :].rearrange("(t p) d -> p t d", p=P),
                             zeros.unsqueeze(1).to_broadcast([P, 3, D])).then_inc(pads_set, 16)
            for h in range(2, HEADS):
                sp.wait_ge(fill_done, fill_of[("V", h - 2, 3)] + 1)
                sp.dma_start(ctxT[:, h % 2, :], io["ctxT"][h * P:(h + 1) * P, :]).then_inc(ctx_in[h], 16)
            for i in range(TILES):
                sp.wait_ge(xn2_ready, i + 1)
                sp.dma_start(io["xn2"][i * P:(i + 1) * P, :], xn[:, i % 2, :]).then_inc(xn2_out[i % 2], 16)
            sp.wait_ge(xn2_out[0], 16 * TILES // 2)
            sp.wait_ge(xn2_out[1], 16 * TILES // 2)

        @block.gpsimd
        def _(pool):
            nc.gpsimd.memset(zeros, 0.0).then_inc(pad_zero, 1)
            nc.gpsimd.memset(neg_half[:, :], -0.5).then_inc(half_set, 1)
            pool.wait_ge(half_set, 1)
            for n, (slot, eps) in enumerate(slot_order):
                pool.wait_ge(mv_ready, n + 1)
                nc.gpsimd.tensor_scalar(var_eps[:, slot:slot + 1], mv[:, slot, 1:2], eps, None,
                                        ALU.add).then_inc(var_ready, 1)
                pool.wait_ge(var_ready, n + 1)
                nc.gpsimd.tensor_tensor(rstd[:, slot:slot + 1], var_eps[:, slot:slot + 1], neg_half[:, :],
                                        ALU.pow).then_inc(rstd_ready, 1)

        @block.scalar
        def _(act):
            act.dma_start(keep["gates"][:, 0:1], io["g_xattn"].to_broadcast([P, 1])).then_inc(gate_in, 16)
            act.dma_start(keep["gates"][:, 1:2], io["g_ffn"].to_broadcast([P, 1])).then_inc(gate_in, 16)
            act.wait_ge(gate_in, 32)
            nc.scalar.activation(keep["tanh"][:, :], keep["gates"][:, :], ACT.Tanh).then_inc(gates_ready, 1)
            for i in range(TILES):
                act.wait_ge(xn_turned, i + 1)
                nc.scalar.activation(xnT[:, :, i * P:(i + 1) * P],
                                     (T0, T1)[i % 2][:, :].rearrange("p (k n) -> p k n", k=KD),
                                     ACT.Copy).then_inc(xnT_ready, 1)
            for item in plan:
                r = fill_of.get(item)
                if r is not None and r % 2 == 0:
                    if item == ("O", 0, 0):
                        act.wait_ge(pads_set, 16 * ROUTED // 3)
                    act.wait_ge(fill_done, r + 1)
                    nc.scalar.activation(destination(*item), source(item[0], ring[r % 4]),
                                         ACT.Copy).then_inc(act_evac, 1)
            for t in range(TILES + 5):
                i = t - 1
                if 0 <= i < TILES:
                    act.wait_ge(z_turned, i + 1)
                    if i >= 2:
                        act.wait_ge(wo_done, i - 1)
                    nc.scalar.activation(ZT[:, i % 2, :, :], (T0, T1)[i % 2][:, :].rearrange("p (k n) -> p k n", k=KD),
                                         ACT.Copy).then_inc(zT_ready, 1)
                i = t - 4
                if 0 <= i < TILES:
                    act.wait_ge(xn2_turned, i + 1)
                    if i >= 2:
                        act.wait_ge(logits_done, i - 1)
                    nc.scalar.activation(xn2T[:, i % 2, :, :], P2[:, :].rearrange("p (k n) -> p k n", k=KD),
                                         ACT.Copy).then_inc(xn2T_ready, 1)

        @block.tensor
        def _(pe):
            pe.wait_ge(ident_in, 16)
            for i in range(TILES):
                pe.wait_ge(xn_ready, i + 1)
                if i >= 2:
                    pe.wait_ge(xnT_ready, i - 1)
                for k in range(KD):
                    last = nc.tensor.transpose((T0, T1)[i % 2][:, k * P:(k + 1) * P],
                                               xn[:, i % 2, k * P:(k + 1) * P], ident[:, :])
                last.then_inc(xn_turned, 1)
            pe.wait_ge(wh_in, 16)
            pe.wait_ge(xnT_ready, TILES)
            for kind, h, c in plan:
                if kind == "S":
                    pe.wait_ge(act_evac, (fill_of[("V", h, 3)] + 1) // 2)
                    pe.wait_ge(dve_evac, (fill_of[("V", h, 3)] + 1) // 2)
                    if h:
                        pe.wait_ge(at_ready, 2 * h)
                    for tc in range(2):
                        for b in range(B):
                            last = nc.tensor.matmul((S0, S1)[tc][:, 0:S],
                                                    KT[:, h % 2, b * S + tc * P:b * S + tc * P + P],
                                                    QT[:, h % 2, b * S:(b + 1) * S],
                                                    start=(b == 0), stop=(b == B - 1))
                        last.then_inc(s_done, 1)
                    continue
                r = fill_of[(kind, h, c)]
                if r >= 4:
                    pe.wait_ge((act_evac, dve_evac)[r % 2], (r - 4) // 2 + 1)
                bank = ring[r % 4]
                if kind == "Q":
                    last = nc.tensor.matmul(bank[:, :], wh[:, h, :], xnT[:, h, c * 512:(c + 1) * 512],
                                            start=True, stop=True)
                elif kind == "K":
                    pe.wait_ge(ctx_in[h], 16)
                    last = nc.tensor.matmul(bank[:, :], wh[:, h, :], ctxT[:, h % 2, c * 512:(c + 1) * 512],
                                            start=True, stop=True)
                elif kind == "V":
                    for q in range(4):
                        n0 = (4 * c + q) * P
                        last = nc.tensor.matmul(bank[:, q * P:(q + 1) * P], ctxT[:, h % 2, n0:n0 + P],
                                                wh[:, h, :], start=True, stop=True)
                else:
                    pe.wait_ge(at_ready, 2 * h + 2)
                    sc, bg = c // 2, c % 2
                    for tc in range(2):
                        last = nc.tensor.matmul(bank[:, :], AT[:, h % 2, tc, sc * P:(sc + 1) * P],
                                                V[:, h % 2, tc, 4 * bg:4 * bg + 4, :],
                                                start=(tc == 0), stop=(tc == 1))
                last.then_inc(fill_done, 1)
            pe.wait_ge(act_evac, r // 2 + 1)
            pe.wait_ge(dve_evac, r // 2 + 1)
            for t in range(TILES + 5):
                i = t
                if i < TILES:
                    if i == 0:
                        pe.wait_ge(wg_in, 16)
                    if i >= 2:
                        pe.wait_ge(z_ready, i - 1)
                    for k in range(KD):
                        last = nc.tensor.matmul((P0, P1)[i % 2][:, :], xnT[:, k, i * P:(i + 1) * P], wg[:, k, :],
                                                start=(k == 0), stop=(k == KD - 1))
                    last.then_inc(w_done, 1)
                i = t - 1
                if 0 <= i < TILES:
                    pe.wait_ge(z_ready, i + 1)
                    if i >= 2:
                        pe.wait_ge(zT_ready, i - 1)
                    for k in range(KD):
                        last = nc.tensor.transpose((T0, T1)[i % 2][:, k * P:(k + 1) * P],
                                                   Z[:, i % 2, k * P:(k + 1) * P], ident[:, :])
                    last.then_inc(z_turned, 1)
                i = t - 2
                if 0 <= i < TILES:
                    if i == 0:
                        pe.wait_ge(wo_in, 16)
                        pe.wait_ge(at_ready, 2 * HEADS)
                    pe.wait_ge(zT_ready, i + 1)
                    if i >= 2:
                        pe.wait_ge(mv_ready, turn_of[2 * TILES + i - 2] + 1)
                    for k in range(KD):
                        last = nc.tensor.matmul((S0, S1)[i % 2][:, :], ZT[:, i % 2, k, :], wo[:, k, :],
                                                start=(k == 0), stop=(k == KD - 1))
                    last.then_inc(wo_done, 1)
                i = t - 4
                if 0 <= i < TILES:
                    pe.wait_ge(xn2_ready, i + 1)
                    if i >= 1:
                        pe.wait_ge(xn2T_ready, i)
                    for k in range(KD):
                        last = nc.tensor.transpose(P2[:, k * P:(k + 1) * P], xn[:, i % 2, k * P:(k + 1) * P],
                                                   ident[:, :])
                    last.then_inc(xn2_turned, 1)
                i = t - 5
                if 0 <= i < TILES:
                    if i == 0:
                        pe.wait_ge(wr_in, 16)
                    pe.wait_ge(xn2T_ready, i + 1)
                    for k in range(KD):
                        last = nc.tensor.matmul(P3[:, i * E:(i + 1) * E], xn2T[:, i % 2, k, :], wr[:, k, :],
                                                start=(k == 0), stop=(k == KD - 1))
                    last.then_inc(logits_done, 1)

        @block.vector
        def _(dve):
            count = [0]

            def link(ins):
                count[0] += 1
                ins.then_inc(dve_step, 1)
                dve.wait_ge(dve_step, count[0])

            def moments(src, slot):
                link(nc.vector.bn_stats(stats[:, slot, :], src))
                nc.vector.bn_aggr(mv[:, slot, :], stats[:, slot, :]).then_inc(mv_ready, 1)

            def normalised(out, src, slot):
                dve.wait_ge(mv_ready, turn_of[slot] + 1)
                dve.wait_ge(rstd_ready, turn_of[slot] + 1)
                return nc.vector.tensor_scalar(out, src, mv[:, slot, 0:1], rstd[:, slot:slot + 1],
                                               ALU.subtract, ALU.mult)

            for t in range(TILES + 2):
                if t < TILES:
                    if t % 4 == 0:
                        dve.wait_ge(x_in[t // 4], 16)
                    moments(x[:, t, :], t)
                i = t - 2
                if i >= 0:
                    if i >= 2:
                        dve.wait_ge(xn_turned, i - 1)
                    normalised(xn[:, i % 2, :], x[:, i, :], i).then_inc(xn_ready, 1)
            dve.wait_ge(mask_in, 16)
            for item in plan:
                if item[0] == "S":
                    h = item[1]
                    for tc in range(2):
                        if h or tc:
                            dve.wait_ge(at_ready, 2 * h + tc)
                        dve.wait_ge(s_done, 2 * h + tc + 1)
                        link(nc.vector.tensor_tensor(masked[:, :], (S0, S1)[tc][:, 0:S], mask[:, h, tc, :], ALU.mult))
                        link(nc.vector.tensor_scalar(AT[:, h % 2, tc, :], masked[:, :], -1.0, 1.0, ALU.mult, ALU.max))
                        nc.vector.tensor_tensor(AT[:, h % 2, tc, :], AT[:, h % 2, tc, :], masked[:, :],
                                                ALU.max).then_inc(at_ready, 1)
                    continue
                r = fill_of[item]
                if r % 2:
                    if item == ("O", 0, 1):
                        dve.wait_ge(pads_set, 16 * ROUTED // 3)
                    dve.wait_ge(fill_done, r + 1)
                    nc.vector.tensor_copy(destination(*item), source(item[0], ring[r % 4])).then_inc(dve_evac, 1)
            dve.wait_ge(act_evac, (len(fill_of) + 1) // 2)
            dve.wait_ge(dve_evac, len(fill_of) // 2)
            dve.wait_ge(gb_in, 32)
            dve.wait_ge(gates_ready, 1)

            def o_rows(i):
                return O[:, i % 2, i // 2, :, :].rearrange("p h e -> p (h e)")

            moments(o_rows(0), TILES)
            moments(o_rows(1), TILES + 1)
            for t in range(TILES + 3):
                if t + 2 < TILES:
                    moments(o_rows(t + 2), TILES + t + 2)
                i = t
                if i < TILES:
                    if i:
                        dve.wait_ge(z_ready, i)
                    link(normalised(Y, o_rows(i), TILES + i))
                    link(nc.vector.tensor_tensor(Y, Y, gamma[:, :], ALU.mult))
                    link(nc.vector.tensor_tensor(Y, Y, beta[:, :], ALU.add))
                    dve.wait_ge(w_done, i + 1)
                    if i >= 2:
                        dve.wait_ge(z_turned, i - 1)
                    nc.vector.scalar_tensor_tensor(Z[:, i % 2, :], (P0, P1)[i % 2][:, :], 0.0, Y,
                                                   ALU.max, ALU.mult).then_inc(z_ready, 1)
                i = t - 2
                if 0 <= i < TILES:
                    dve.wait_ge(wo_done, i + 1)
                    link(nc.vector.scalar_tensor_tensor(x[:, i, :], (S0, S1)[i % 2][:, :], keep["tanh"][:, 0:1],
                                                        x[:, i, :], ALU.mult, ALU.add))
                    moments(x[:, i, :], 2 * TILES + i)
                i = t - 3
                if 0 <= i < TILES:
                    if i >= 2:
                        dve.wait_ge(xn2_turned, i - 1)
                        dve.wait_ge(xn2_out[i % 2], 16 * (i // 2))
                    normalised(xn[:, i % 2, :], x[:, i, :], 2 * TILES + i).then_inc(xn2_ready, 1)

            dve.wait_ge(logits_done, TILES)
            nc.vector.tensor_copy(keep["logits"][:, :], P3[:, 0:TILES * E]).then_inc(dve_step, 1)


UP_SPANS = [(0, 228), (228, 227), (455, 227)]
UP_COLS = 2 * HID
DOWN_AT = KD * UP_COLS
WIDTH = DOWN_AT + (HC + 1) * D
PIECES = ([(k * UP_COLS, UP_COLS, P) for k in range(KD)]
          + [(DOWN_AT, 2 * D, P), (DOWN_AT + 2 * D, 2 * D, P), (DOWN_AT + 4 * D, D, P), (DOWN_AT + HC * D, D, HT)])
NP = len(PIECES)
RAW = UP_COLS
ORDER = [E] + list(range(E)) + [E]
PARTS = ((1, 0), (0, 1), (0, 0))


def route_and_feed_forward(nc, io, keep, banks):
    ctx = ExitStack()
    with ctx:
        def sb(name, shape, dt=F32):
            return ctx.enter_context(nc.sbuf_tensor(name, shape, dt))

        def sem(name):
            return ctx.enter_context(nc.semaphore(name))

        ident = keep["ident"]
        raw = sb("raw", [P, 2, RAW])
        w = [sb(f"w_{x}", [P, 2, WIDTH], F32R) for x in ("hi", "lo")]
        xg = sb("xg", [P, D])
        xT = [sb(f"xT_{x}", [P, KD, P], F32R) for x in ("hi", "lo")]
        hid = sb("hid", [P, (HC + 1) * P])
        hT = [sb(f"hT_{x}", [P, HC + 1, P], F32R) for x in ("hi", "lo")]
        sil = sb("sil", [P, 3, UP_SPANS[0][1]])
        out_sb = sb("out_sb", [P, D])
        rows = sb("rows", [P, 4, D])
        spare = rows[:, 2:4, :].rearrange("p a d -> p (a d)")
        lt = spare[:, 0:5 * TILES * E].rearrange("p (r n) -> p r n", r=5)
        tri = spare[:, 5 * TILES * E:5 * TILES * E + 2 * P].rearrange("p (r n) -> p r n", r=2)
        thr = out_sb[:, 0:ROUTED * (E - 1)]
        small = sb("small", [P, 5, TILES])
        cst = sb("cst", [P, E + E * THR + ROUTED])
        ends = sb("ends", [P, 2, E])
        expert = sb("expert", [P, ROUTED])
        gate_of = sb("gate_of", [P, 2, TILES])
        slot = sb("slot", [P, 2 * TILES], I32)
        parity = sb("parity", [P, ROUTED], I32)
        needs = sb("needs", [P, ROUTED], I32)
        free_at = sb("free_at", [P, E - 1], I32)

        up_bank, hturn_bank, xturn_bank, down_bank, rank_bank = banks[0:3], banks[3:5], banks[5], banks[6], banks[7]

        raw_in = [sem(f"raw_in{q}") for q in range(2)]
        raw_free = [sem(f"raw_free{q}") for q in range(2)]
        buffer_free = sem("buffer_free")
        zeroed, hi0, first_ready, hi_split, split = sem("zeroed"), sem("hi0"), sem("first_ready"), sem("hi_split"), sem("split")
        x_in, x_turned, x_hi, x_lo = sem("x_in"), sem("x_turned"), sem("x_hi"), sem("x_lo")
        up_done, silu_done, h_done = sem("up_done"), sem("silu_done"), sem("h_done")
        h_turned, h_hi, h_lo = sem("h_turned"), sem("h_hi"), sem("h_lo")
        down_done, down_taken, out_ready, stored = sem("down_done"), sem("down_taken"), sem("out_ready"), sem("stored")
        cst_in, dve_step, shifted, exped, chosen, ranked = (sem("cst_in"), sem("dve_step"), sem("shifted"),
                                                           sem("exped"), sem("chosen"), sem("ranked"))
        slots_ready, tables_ready = sem("slots_ready"), sem("tables_ready")
        tile_in = [sem(f"tile_in{q}") for q in range(4)]
        tile_out = [sem(f"tile_out{q}") for q in range(4)]
        row_in = [sem(f"row_in{q}") for q in range(2)]
        row_added, y_out = sem("row_added"), sem("y_out")
        block = ctx.enter_context(nc.Block())

        shared_tile = list(range(FIRST)) + [None] * ROUTED + list(range(FIRST, TILES))

        def part(q, buf, piece):
            c0, n, rows_ = PIECES[piece]
            return w[q][0:rows_, buf, c0:c0 + n]

        def added_in(m):
            return range((m - 1) * TILES // LAST, m * TILES // LAST)

        def complete_at(i):
            return max(i - FIRST + 1, next(m for m in range(1, LAST + 1) if i in added_in(m)))

        @block.sync
        def _(sp):
            def load(version, piece):
                n = version * NP + piece
                if n >= 2:
                    sp.wait_ge(raw_free[n % 2], n // 2)
                e, (c0, cols, rows_) = ORDER[version], PIECES[piece]
                if c0 < DOWN_AT:
                    src = io["w_up"][e, :, c0 // UP_COLS, :]
                elif rows_ == P:
                    j = (c0 - DOWN_AT) // D
                    src = io["w_down"][e, :, j:j + cols // D, :].rearrange("p j d -> p (j d)")
                else:
                    src = io["w_downt"][e, :, :]
                sp.dma_start(raw[0:rows_, n % 2, 0:cols], src).then_inc(raw_in[n % 2], 16)

            for piece in range(NP):
                load(0, piece)
            sp.dma_start(tri[:, :, :], io["tri"]).then_inc(cst_in, 16)
            sp.dma_start(cst[:, :], io["cst"]).then_inc(cst_in, 16)
            for piece in range(NP):
                load(1, piece)
            for i in range(TILES):
                if i == 2:
                    sp.wait_ge(slots_ready, 2)
                if i >= 4:
                    sp.wait_ge(tile_out[i % 4], 32 * (i // 4))
                sp.dma_start(rows[:, i % 4, :], io["xn2"][i * P:(i + 1) * P, :]).then_inc(tile_in[i % 4], 16)
            for version in range(2, len(ORDER)):
                for piece in range(NP):
                    load(version, piece)

        @block.gpsimd
        def _(pool):
            def split_version(version):
                for piece in range(NP):
                    n = version * NP + piece
                    c0, cols, rows_ = PIECES[piece]
                    src = raw[0:rows_, n % 2, 0:cols]
                    pool.wait_ge(raw_in[n % 2], 16 * (n // 2 + 1))
                    nc.gpsimd.tensor_copy(part(0, version % 2, piece), src).then_inc(hi_split, 1)
                    pool.wait_ge(hi_split, n - NP + 1)
                    nc.gpsimd.tensor_tensor(part(1, version % 2, piece), src, part(0, version % 2, piece).bitcast(F32),
                                            ALU.subtract).then_inc(split, 1)
                    pool.wait_ge(split, n - NP + 1)
                    pool.sem_inc(raw_free[n % 2], 1)

            pool.wait_ge(zeroed, 5)
            split_version(1)
            pool.wait_ge(slots_ready, 2)
            for i in range(TILES):
                pool.wait_ge(tile_in[i % 4], 16 * (i // 4 + 1))
                for c in range(2):
                    nc.gpsimd.indirect_dma_start(
                        out=io["slots"], out_offset=bass.IndirectOffsetOnAxis(slot[:, c * TILES + i:c * TILES + i + 1], 0),
                        in_=rows[:, i % 4, :], in_offset=None).then_inc(tile_out[i % 4], 16)
            pool.wait_ge(down_done, FIRST)
            split_version(2)
            pool.wait_ge(tables_ready, 1)
            for version in range(3, len(ORDER)):
                done = pool.value_load(free_at[0:1, version - 3:version - 2], min_val=FIRST + 1, max_val=FIRST + ROUTED)
                pool.wait_ge(down_done, done)
                pool.sem_inc(buffer_free, 1)
                pool.wait_ge(buffer_free, version - 2)
                split_version(version)
            pool.wait_ge(stored, 16 * ROUTED)
            for i in range(TILES):
                if i >= 2:
                    pool.wait_ge(row_added, 2 * (i - 1))
                for c in range(2):
                    nc.gpsimd.indirect_dma_start(
                        out=rows[:, 2 * (i % 2) + c, :], out_offset=None, in_=io["routed"],
                        in_offset=bass.IndirectOffsetOnAxis(slot[:, c * TILES + i:c * TILES + i + 1], 0)
                    ).then_inc(row_in[i % 2], 16)

        @block.scalar
        def _(act):
            def load_x(s, loop=None):
                if loop is not None:
                    act.dma_start(xg[:, :], io["slots"][bass.ds(loop * P, P), :]).then_inc(x_in, 16)
                    return
                if s >= STEPS:
                    return
                if s == FIRST:
                    for q in range(4):
                        act.wait_ge(tile_out[q], 32 * TILES // 4)
                i = shared_tile[s]
                src = io["slots"][(s - FIRST) * P:(s - FIRST + 1) * P, :] if i is None else io["xn2"][i * P:(i + 1) * P, :]
                act.dma_start(xg[:, :], src).then_inc(x_in, 16)

            def x_high(s):
                act.wait_ge(x_turned, s + 1)
                nc.scalar.activation(xT[0][:, :, :], xturn_bank[:, :].rearrange("p (k n) -> p k n", k=KD),
                                     ACT.Copy).then_inc(x_hi, 1)

            def h_high(s):
                for q, (a, b) in enumerate(((0, 4), (4, 6))):
                    act.wait_ge(h_turned, 2 * s + q + 1)
                    nc.scalar.activation(hT[0][:, a:b, :], hturn_bank[q][:, 0:(b - a) * P].rearrange("p (k n) -> p k n", k=b - a),
                                         ACT.Copy).then_inc(h_hi, 1)

            def iteration(s, up=True, turn=True, down=True, routed_down=False, loop=None):
                for c in range(3):
                    if up:
                        n = UP_SPANS[c][1]
                        act.wait_ge(up_done, 3 * s + c + 1)
                        nc.scalar.activation(sil[:, c, 0:n], up_bank[c][:, 0:n], ACT.Silu).then_inc(silu_done, 1)
                    if c == 0 and down:
                        h_high(s - 1)
                if turn:
                    x_high(s + 1)
                    load_x(s + 2, None if loop is None else loop + 2)
                if down and routed_down:
                    act.wait_ge(down_done, s)
                    m = s - FIRST
                    if loop is not None or m > 1:
                        act.wait_ge(stored, 16 * (m - 1))
                    nc.scalar.activation(out_sb[:, :], down_bank[:, :], ACT.Copy).then_inc(out_ready, 1)
                    act.wait_ge(out_ready, m + 1)
                    dst = io["routed"][(m - 1) * P:m * P, :] if loop is None else io["routed"][bass.ds((loop - 1) * P, P), :]
                    act.dma_start(dst, out_sb[:, :]).then_inc(stored, 16)

            load_x(0)
            act.wait_ge(zeroed, 5)
            for piece in range(NP):
                c0, cols, rows_ = PIECES[piece]
                act.wait_ge(raw_in[piece % 2], 16 * (piece // 2 + 1))
                nc.scalar.activation(part(0, 0, piece), raw[0:rows_, piece % 2, 0:cols], ACT.Copy).then_inc(hi0, 1)
            x_high(0)
            load_x(1)
            act.wait_ge(shifted, 1)
            nc.scalar.activation(lt[:, 1, :], lt[:, 0, :], ACT.Exp).then_inc(exped, 1)
            for s in range(FIRST + 2):
                if s == FIRST + 1:
                    act.wait_ge(down_taken, FIRST)
                    act.wait_ge(tables_ready, 1)
                    act.sem_inc(out_ready, 1)
                iteration(s, down=s > 0, routed_down=s > FIRST)
            with act.Fori(2, ROUTED - 2) as r:
                iteration(r + FIRST, routed_down=True, loop=r)
            for s in range(FIRST + ROUTED - 2, STEPS + 1):
                iteration(s, up=s < STEPS, turn=s + 1 < STEPS, routed_down=s <= FIRST + ROUTED)
                m = s - FIRST - ROUTED
                for i in range(TILES):
                    if m > 0 and complete_at(i) == m:
                        act.wait_ge(down_taken, FIRST + m)
                        act.wait_ge(row_added, 2 * i + 2)
                        act.dma_start(io["out"][i * P:(i + 1) * P, :], keep["x"][:, i, :]).then_inc(y_out, 16)
            act.wait_ge(y_out, 16 * TILES)

        @block.tensor
        def _(pe):
            def turn_x(s):
                pe.wait_ge(x_in, 16 * (s + 1))
                if not isinstance(s, int) or s:
                    pe.wait_ge(x_lo, s)
                for k in range(KD):
                    mm = nc.tensor.transpose(xturn_bank[:, k * P:(k + 1) * P], xg[:, k * P:(k + 1) * P], ident[:, :])
                mm.then_inc(x_turned, 1)

            def moving(q, buf, c0, n):
                if isinstance(buf, int):
                    return w[q][:, buf, c0:c0 + n]
                return w[q][:, bass.ds(buf, 1), c0:c0 + n].rearrange("p o n -> p (o n)")

            def up(s, c, buf):
                c0 = 2 * UP_SPANS[c][0]
                n = 2 * UP_SPANS[c][1]
                if not isinstance(s, int) or s:
                    pe.wait_ge(h_done, 3 * s + c - 2)
                for g, (a, b) in enumerate(PARTS):
                    for k in range(KD):
                        mm = nc.tensor.matmul(up_bank[c][:, 0:n], xT[a][:, k, :], moving(b, buf, k * UP_COLS + c0, n),
                                              start=(g == 0 and k == 0), stop=(g == 2 and k == KD - 1))
                mm.then_inc(up_done, 1)

            def turn_h(s):
                pe.wait_ge(h_done, 3 * s + 3)
                if not isinstance(s, int) or s:
                    pe.wait_ge(h_lo, 2 * s)
                for j in range(HC + 1):
                    mm = nc.tensor.transpose(hturn_bank[j // 4][:, (j % 4) * P:(j % 4 + 1) * P], hid[:, j * P:(j + 1) * P],
                                             ident[:, :])
                    if j in (3, HC):
                        mm.then_inc(h_turned, 1)

            def down(s, buf, taken, n_taken):
                pe.wait_ge(h_lo, 2 * s + 2)
                if taken is not None:
                    pe.wait_ge(taken, n_taken)
                for j in range(HC + 1):
                    for g, (a, b) in enumerate(PARTS):
                        mm = nc.tensor.matmul(down_bank[:, :], hT[a][:, j, :], moving(b, buf, DOWN_AT + j * D, D),
                                              start=(j == 0 and g == 0), stop=(j == HC and g == 2))
                mm.then_inc(down_done, 1)

            turn_x(0)
            pe.wait_ge(first_ready, NP)
            pe.wait_ge(cst_in, 32)
            for s in range(FIRST + 1):
                pe.wait_ge(x_lo, s + 1)
                if s == FIRST:
                    pe.wait_ge(split, NP)
                buf = s // FIRST
                up(s, 0, buf)
                if s:
                    turn_h(s - 1)
                up(s, 1, buf)
                up(s, 2, buf)
                turn_x(s + 1)
                if s:
                    down(s - 1, 0, down_taken if s > 1 else None, s - 1)
                if s == 0:
                    pe.wait_ge(chosen, 1)
                    nc.tensor.matmul(rank_bank[:, 0:TILES * E], tri[:, 0, :], lt[:, 4, :], start=True, stop=True)
                    nc.tensor.matmul(rank_bank[:, TILES * E:2 * TILES * E], tri[:, 1, :], lt[:, 4, :], start=True,
                                     stop=True).then_inc(ranked, 1)
            pe.wait_ge(tables_ready, 1)
            with pe.Fori(1, ROUTED - 1) as r:
                buf = pe.value_load(parity[0:1, bass.ds(r, 1)], min_val=0, max_val=1)
                buf_before = pe.value_load(parity[0:1, bass.ds(r - 1, 1)], min_val=0, max_val=1)
                need = pe.value_load(needs[0:1, bass.ds(r, 1)], min_val=NP, max_val=NP * E)
                s = r + FIRST
                pe.wait_ge(split, need)
                pe.wait_ge(x_lo, s + 1)
                up(s, 0, buf)
                turn_h(s - 1)
                up(s, 1, buf)
                up(s, 2, buf)
                turn_x(s + 1)
                down(s - 1, buf_before, out_ready, r)
            for s in range(FIRST + ROUTED - 1, STEPS + 1):
                m = s - FIRST - ROUTED
                if s < STEPS:
                    pe.wait_ge(x_lo, s + 1)
                    buf = 0 if m < 0 else 1
                    pe.wait_ge(split, NP * (E + (m >= 0)))
                    up(s, 0, buf)
                turn_h(s - 1)
                if s < STEPS:
                    up(s, 1, buf)
                    up(s, 2, buf)
                if s + 1 < STEPS:
                    turn_x(s + 1)
                if m == -1:
                    before = pe.value_load(parity[0:1, ROUTED - 2:ROUTED - 1], min_val=0, max_val=1)
                    down(s - 1, before, out_ready, s - FIRST)
                elif m <= 1:
                    down(s - 1, m, out_ready, s - FIRST)
                else:
                    down(s - 1, 1, down_taken, FIRST + m - 1)

        @block.vector
        def _(dve):
            count = [0]

            def link(ins):
                count[0] += 1
                ins.then_inc(dve_step, 1)
                dve.wait_ge(dve_step, count[0])

            for q in range(2):
                for buf in range(2):
                    nc.vector.memset(w[q][:, buf, DOWN_AT + HC * D:WIDTH].bitcast(F32), 0.0).then_inc(zeroed, 1)
            nc.vector.memset(hid[:, HID:(HC + 1) * P], 0.0).then_inc(zeroed, 1)
            dve.wait_ge(zeroed, 5)

            def x_low(s):
                dve.wait_ge(x_hi, s + 1)
                nc.vector.tensor_tensor(xT[1][:, :, :], xturn_bank[:, :].rearrange("p (k n) -> p k n", k=KD),
                                        xT[0][:, :, :].bitcast(F32), ALU.subtract).then_inc(x_lo, 1)

            def iteration(s, up=True, turn=True, down=True, add_shared=None):
                for c in range(3):
                    if up:
                        h0, n = UP_SPANS[c]
                        dve.wait_ge(silu_done, 3 * s + c + 1)
                        if down:
                            dve.wait_ge(h_turned, 2 * s)
                        nc.vector.tensor_tensor(hid[:, h0:h0 + n], sil[:, c, 0:n], up_bank[c][:, n:2 * n],
                                                ALU.mult).then_inc(h_done, 1)
                    if c == 0 and down:
                        for q, (a, b) in enumerate(((0, 4), (4, 6))):
                            dve.wait_ge(h_hi, 2 * (s - 1) + q + 1)
                            nc.vector.tensor_tensor(hT[1][:, a:b, :],
                                                    hturn_bank[q][:, 0:(b - a) * P].rearrange("p (k n) -> p k n", k=b - a),
                                                    hT[0][:, a:b, :].bitcast(F32), ALU.subtract).then_inc(h_lo, 1)
                if turn:
                    x_low(s + 1)
                if add_shared is not None:
                    i = add_shared
                    dve.wait_ge(down_done, s)
                    nc.vector.scalar_tensor_tensor(keep["x"][:, i, :], down_bank[:, :], keep["tanh"][:, 1:2],
                                                   keep["x"][:, i, :], ALU.mult, ALU.add).then_inc(down_taken, 1)

            def by_expert(n):
                return lt[:, n, :].rearrange("p (t e) -> p t e", e=E)

            def over(ap):
                return ap.unsqueeze(2).to_broadcast([P, TILES, E])

            logits = keep["logits"][:, :].rearrange("p (t e) -> p t e", e=E)
            experts = cst[:, 0:E].unsqueeze(1).to_broadcast([P, TILES, E])

            def softmax_shift():
                link(nc.vector.tensor_reduce(small[:, 0, :], logits, X, ALU.max))
                nc.vector.tensor_tensor(by_expert(0), logits, over(small[:, 0, :]), ALU.subtract).then_inc(shifted, 1)

            def choose():
                dve.wait_ge(exped, 1)
                link(nc.vector.tensor_reduce(small[:, 1, :], by_expert(1), X, ALU.add))
                link(nc.vector.reciprocal(small[:, 1, :], small[:, 1, :]))
                link(nc.vector.tensor_tensor(by_expert(1), by_expert(1), over(small[:, 1, :]), ALU.mult))
                dve.wait_ge(cst_in, 32)
                for c in range(2):
                    onehot = by_expert(2 + c)
                    link(nc.vector.tensor_reduce(small[:, 2 + c, :], by_expert(1), X, ALU.max))
                    link(nc.vector.tensor_tensor(by_expert(0), by_expert(1), over(small[:, 2 + c, :]), ALU.is_equal))
                    link(nc.vector.tensor_tensor(by_expert(0), by_expert(0), experts, ALU.mult))
                    link(nc.vector.tensor_reduce(small[:, 4, :], by_expert(0), X, ALU.min))
                    link(nc.vector.tensor_tensor(onehot, over(small[:, 4, :]), experts, ALU.is_equal))
                    if c == 0:
                        link(nc.vector.scalar_tensor_tensor(lt[:, 1, :], lt[:, 2, :], -2.0, lt[:, 1, :], ALU.mult, ALU.add))
                nc.vector.tensor_tensor(lt[:, 4, :], lt[:, 2, :], lt[:, 3, :], ALU.add).then_inc(chosen, 1)

            def weigh():
                link(nc.vector.tensor_tensor(small[:, 4, :], small[:, 2, :], small[:, 3, :], ALU.add))
                link(nc.vector.reciprocal(small[:, 4, :], small[:, 4, :]))
                link(nc.vector.tensor_scalar(small[:, 4, :], small[:, 4, :], keep["tanh"][:, 1:2], None, ALU.mult))
                for c in range(2):
                    link(nc.vector.tensor_tensor(gate_of[:, c, :], small[:, 2 + c, :], small[:, 4, :], ALU.mult))

            def place():
                dve.wait_ge(ranked, 1)
                rank, total = rank_bank[:, 0:TILES * E], rank_bank[:, TILES * E:2 * TILES * E]
                link(nc.vector.tensor_copy(lt[:, 0, :], total))
                a, b, d = 0, 1, 1
                while d < TILES:
                    link(nc.vector.tensor_copy(lt[:, b, 0:d * E], lt[:, a, 0:d * E]))
                    link(nc.vector.tensor_tensor(lt[:, b, d * E:], lt[:, a, d * E:], lt[:, a, 0:(TILES - d) * E], ALU.add))
                    a, b, d = b, a, 2 * d
                counts = lt[:, a, (TILES - 1) * E:TILES * E]
                over_thr = thr[:, 0:E * THR].rearrange("p (e k) -> p e k", k=THR)
                link(nc.vector.tensor_tensor(over_thr, counts.unsqueeze(2).to_broadcast([P, E, THR]),
                                             cst[:, E:E + E * THR].rearrange("p (e k) -> p e k", k=THR), ALU.is_gt))
                link(nc.vector.tensor_reduce(ends[:, 0, :], over_thr, X, ALU.add))
                u, v, d = 0, 1, 1
                while d < E:
                    link(nc.vector.tensor_copy(ends[:, v, 0:d], ends[:, u, 0:d]))
                    link(nc.vector.tensor_tensor(ends[:, v, d:E], ends[:, u, d:E], ends[:, u, 0:E - d], ALU.add))
                    u, v, d = v, u, 2 * d
                link(nc.vector.tensor_tensor(lt[:, 4, :], lt[:, a, :], total, ALU.subtract))
                link(nc.vector.tensor_tensor(lt[:, 4, :], lt[:, 4, :], rank, ALU.add))
                link(nc.vector.memset(ends[:, v, 0:1], 0.0))
                link(nc.vector.tensor_scalar(ends[:, v, 1:E], ends[:, u, 0:E - 1], float(P), None, ALU.mult))
                link(nc.vector.tensor_tensor(by_expert(4), by_expert(4),
                                             ends[:, v, :].unsqueeze(1).to_broadcast([P, TILES, E]), ALU.add))
                for c in range(2):
                    link(nc.vector.tensor_tensor(lt[:, 0, :], lt[:, 2 + c, :], lt[:, 4, :], ALU.mult))
                    link(nc.vector.tensor_reduce(small[:, c, :], by_expert(0), X, ALU.add))
                    nc.vector.tensor_copy(slot[:, c * TILES:(c + 1) * TILES], small[:, c, :]).then_inc(slots_ready, 1)
                return ends[:, u, 0:E - 1]

            def tables(end):
                at = thr.rearrange("p (s e) -> p s e", e=E - 1)
                link(nc.vector.tensor_tensor(at, end.unsqueeze(1).to_broadcast([P, ROUTED, E - 1]),
                                             cst[:, E + E * THR:].unsqueeze(2).to_broadcast([P, ROUTED, E - 1]), ALU.is_le))
                link(nc.vector.tensor_reduce(expert[:, :], at, X, ALU.add))
                link(nc.vector.tensor_scalar(needs[:, :], expert[:, :], float(NP), float(NP), ALU.mult, ALU.add))
                link(nc.vector.tensor_scalar(expert[:, :], expert[:, :], 1.0, None, ALU.add))
                link(nc.vector.tensor_copy(parity[:, :], expert[:, :]))
                link(nc.vector.tensor_scalar(parity[:, :], parity[:, :], 1, None, ALU.bitwise_and))
                nc.vector.tensor_scalar(free_at[:, :], end, float(FIRST), None, ALU.add).then_inc(tables_ready, 1)

            for piece in range(NP):
                c0, cols, rows_ = PIECES[piece]
                dve.wait_ge(hi0, piece + 1)
                nc.vector.tensor_tensor(part(1, 0, piece), raw[0:rows_, piece % 2, 0:cols],
                                        part(0, 0, piece).bitcast(F32), ALU.subtract).then_inc(first_ready, 1)
                dve.wait_ge(first_ready, piece + 1)
                dve.sem_inc(raw_free[piece % 2], 1)
            x_low(0)
            softmax_shift()
            for s in range(FIRST + 1):
                if s == 0:
                    choose()
                if s == 1:
                    weigh()
                    end = place()
                if s == 2:
                    tables(end)
                iteration(s, down=s > 0, add_shared=shared_tile[s - 1] if s else None)
            with dve.Fori(1, ROUTED - 1) as r:
                iteration(r + FIRST)
            for s in range(FIRST + ROUTED - 1, STEPS + 1):
                m = s - FIRST - ROUTED
                iteration(s, up=s < STEPS, turn=s + 1 < STEPS)
                if m < 1:
                    continue
                dve.wait_ge(down_taken, FIRST + m - 1)
                for i in added_in(m):
                    dve.wait_ge(row_in[i % 2], 32 * (i // 2 + 1))
                    for c in range(2):
                        nc.vector.scalar_tensor_tensor(keep["x"][:, i, :], rows[:, 2 * (i % 2) + c, :],
                                                       gate_of[:, c, i:i + 1], keep["x"][:, i, :],
                                                       ALU.mult, ALU.add).then_inc(row_added, 1)
                        dve.wait_ge(row_added, 2 * i + c + 1)
                i = shared_tile[s - 1]
                dve.wait_ge(down_done, s)
                nc.vector.scalar_tensor_tensor(keep["x"][:, i, :], down_bank[:, :], keep["tanh"][:, 1:2],
                                               keep["x"][:, i, :], ALU.mult, ALU.add).then_inc(down_taken, 1)


def build(nc, io):
    io["xn2"] = nc.dram_tensor("xn2_rows", (N, D), F32, kind="Internal").ap()
    io["slots"] = nc.dram_tensor("slot_rows", (ROUTED * P, D), F32, kind="Internal").ap()
    io["routed"] = nc.dram_tensor("routed_rows", (ROUTED * P, D), F32, kind="Internal").ap()
    with ExitStack() as ctx:
        def sb(name, shape, dt=F32):
            return ctx.enter_context(nc.sbuf_tensor(name, shape, dt))

        keep = {
            "x": sb("x_all", [P, TILES, D]),
            "ident": sb("ident", [P, P]),
            "gates": sb("gates", [P, 2]),
            "tanh": sb("tanh_gates", [P, 2]),
            "logits": sb("logits", [P, TILES * E]),
        }
        banks = [ctx.enter_context(nc.psum_tensor(f"bank{i}", [P, 512], F32)) for i in range(8)]
        attention(nc, io, keep, banks)
        route_and_feed_forward(nc, io, keep, banks)


def decay_masks():
    gam = 1.0 - 2.0 ** (-5.0 - np.arange(HEADS, dtype=np.float64))
    idx = np.arange(S, dtype=np.float64)
    expo = idx[None, :] - idx[:, None]
    d = np.where(expo[None] <= 0, gam[:, None, None] ** np.minimum(expo, 0)[None], 0.0)
    d = d / np.sqrt(d.sum(-1))[:, None, :] / np.sqrt(float(HD))
    return d.transpose(2, 0, 1).reshape(2, P, HEADS, S).transpose(1, 2, 0, 3).astype(np.float32)


def kernel(**inputs):
    import numpy as _np
    import concourse.bacc as _bacc
    from concourse.bass_utils import run_bass_kernel_spmd as _run

    a = {k: _np.asarray(v) for k, v in inputs.items()}
    w1 = _np.concatenate([a["L0_ffn_ew1"], a["L0_ffn_sw1"][None]]).transpose(0, 2, 1)
    w3 = _np.concatenate([a["L0_ffn_ew3"], a["L0_ffn_sw3"][None]]).transpose(0, 2, 1)
    w2 = _np.concatenate([a["L0_ffn_ew2"], a["L0_ffn_sw2"][None]]).transpose(0, 2, 1)
    parts = []
    for h0, n in UP_SPANS:
        parts += [w1[..., h0:h0 + n], w3[..., h0:h0 + n]]
    up = _np.concatenate(parts, axis=-1).reshape(E + 1, KD, P, 2 * HID)
    cut = HC * P
    limits = _np.arange(THR) * float(P)
    limits[0] = -1.0
    cst = _np.concatenate([_np.arange(E) - 8.0, _np.tile(limits, E),
                           _np.arange(ROUTED, dtype=_np.float64)]).astype(_np.float32)
    arrays = {
        "x": a["x"].reshape(N, D),
        "ctxT": a["ctx_2048"].reshape(N, D).T,
        "wh": a["L0_xattn_Wh"], "wg": a["L0_xattn_wg_w"], "wo": a["L0_xattn_wo_w"],
        "gamma": a["L0_xattn_gn_gamma"].reshape(1, D), "beta": a["L0_xattn_gn_beta"].reshape(1, D),
        "wrT": a["L0_ffn_wr"].T,
        "g_xattn": a["g_xattn"].reshape(1, 1), "g_ffn": a["g_ffn"].reshape(1, 1),
        "w_up": up.transpose(0, 2, 1, 3),
        "w_down": w2[:, :cut].reshape(E + 1, HC, P, D).transpose(0, 2, 1, 3),
        "w_downt": w2[:, cut:],
        "ident": _np.eye(P, dtype=_np.float32),
        "tri": _np.stack([_np.triu(_np.ones((P, P)), 1), _np.ones((P, P))], axis=1).astype(_np.float32),
        "mask": decay_masks(),
        "cst": _np.tile(cst, (P, 1)),
    }
    nc = _bacc.Bacc("TRN2", target_bir_lowering=False, num_devices=1)
    feed, io = {}, {}
    for name, v in arrays.items():
        v = _np.ascontiguousarray(v)
        feed[f"in_{name}"] = v
        io[name] = nc.dram_tensor(f"in_{name}", v.shape, mybir.dt.from_np(v.dtype), kind="ExternalInput").ap()
    io["out"] = nc.dram_tensor("out_y", (N, D), F32, kind="ExternalOutput").ap()
    build(nc, io)
    r = _run(nc, [feed], core_ids=[0])
    return r.results[0]["out_y"].reshape(B, S, D)
```

```python
from contextlib import ExitStack

import numpy as np

import concourse.bass as bass
from concourse import mybir

F32 = mybir.dt.float32
F32R = mybir.dt.float32r
I32 = mybir.dt.int32
ALU = mybir.AluOpType
ACT = mybir.ActivationFunctionType
X = mybir.AxisListType.X

P = 128
B, S, D = 8, 256, 512
HEADS, HD = 4, 128
N = B * S
TILES = N // P
KD = D // P
E = 8
HID = D * 4 // 3
HC = HID // P
HT = HID - HC * P
FIRST = 7
LAST = TILES - FIRST
ROUTED = (2 * N - E) // P + E
STEPS = FIRST + ROUTED + LAST
THR = N // P
EPS1, EPS_GN = 1e-5, 1e-3


def attention(nc, io, keep, banks):
    ctx = ExitStack()
    with ctx:
        def sb(name, shape, dt=F32):
            return ctx.enter_context(nc.sbuf_tensor(name, shape, dt))

        def sem(name):
            return ctx.enter_context(nc.semaphore(name))

        x = keep["x"]
        ident = keep["ident"]
        xn = sb("xn", [P, 2, D])
        xnT = sb("xnT", [P, KD, N])
        ctxT = sb("ctxT", [P, 2, N])
        wh = sb("wh", [P, HEADS, HD])
        wg = sb("wg", [P, KD, D])
        wo = sb("wo", [P, KD, D])
        wr = sb("wr", [P, KD, E])
        mask = sb("mask", [P, HEADS, 2, S])
        gamma = sb("gamma", [P, D])
        beta = sb("beta", [P, D])
        QT = sb("QT", [P, 2, N])
        KT = sb("KT", [P, 2, N])
        V = sb("V", [P, 2, 2, B, HD])
        AT = sb("AT", [P, 2, 2, S])
        masked = sb("masked", [P, S])
        O = sb("O", [P, 2, B, HEADS, HD])
        stats = sb("stats", [P, 3 * TILES, 6])
        mv = sb("mv", [P, 3 * TILES, 2])
        var_eps = sb("var_eps", [P, 3 * TILES])
        rstd = sb("rstd", [P, 3 * TILES])
        neg_half = sb("neg_half", [P, 1])
        Y = QT[:, 0, 0:D]
        Z = QT[:, 0, D:3 * D].rearrange("p (a n) -> p a n", a=2)
        ZT = QT[:, 1, 0:2 * D].rearrange("p (a k n) -> p a k n", a=2, k=KD)
        xn2T = QT[:, 1, 2 * D:4 * D].rearrange("p (a k n) -> p a k n", a=2, k=KD)

        P0, P1, P2, P3, S0, S1, T0, T1 = banks
        ring = [P0, P1, P2, P3]

        x_in = [sem(f"x_in{q}") for q in range(4)]
        ctx_in = [sem(f"ctx_in{h}") for h in range(HEADS)]
        wh_in, mask_in, wg_in, wo_in = sem("wh_in"), sem("mask_in"), sem("wg_in"), sem("wo_in")
        gb_in, wr_in, gate_in, ident_in = sem("gb_in"), sem("wr_in"), sem("gate_in"), sem("ident_in")
        pad_zero, pads_set = sem("pad_zero"), sem("pads_set")
        dve_step = sem("dve_step")
        half_set, mv_ready, var_ready, rstd_ready = (sem("half_set"), sem("mv_ready"), sem("var_ready"),
                                                    sem("rstd_ready"))
        xn_ready, xn_turned, xnT_ready = sem("xn_ready"), sem("xn_turned"), sem("xnT_ready")
        fill_done, act_evac, dve_evac = sem("fill_done"), sem("act_evac"), sem("dve_evac")
        s_done, at_ready = sem("s_done"), sem("at_ready")
        gates_ready = sem("gates_ready")
        w_done, z_ready, z_turned, zT_ready = sem("w_done"), sem("z_ready"), sem("z_turned"), sem("zT_ready")
        wo_done, xn2_ready, xn2_turned, xn2T_ready = (sem("wo_done"), sem("xn2_ready"),
                                                      sem("xn2_turned"), sem("xn2T_ready"))
        xn2_out = [sem(f"xn2_out{q}") for q in range(2)]
        logits_done = sem("logits_done")
        block = ctx.enter_context(nc.Block())

        zeros = O[:, 1, B - 1, :, :].rearrange("p h e -> p (h e)")

        def qkv(h):
            return [(kind, h, c) for kind in "QKV" for c in range(4)]

        plan = qkv(0)
        for h in range(HEADS):
            plan.append(("S", h, 0))
            if h + 1 < HEADS:
                plan += qkv(h + 1)
            plan += [("O", h, c) for c in range(4)]
        fill_of, r = {}, 0
        for item in plan:
            if item[0] != "S":
                fill_of[item] = r
                r += 1

        slot_order = [(i, EPS1) for i in range(TILES)] + [(TILES, EPS_GN), (TILES + 1, EPS_GN)]
        for t in range(TILES + 2):
            if t + 2 < TILES:
                slot_order.append((TILES + t + 2, EPS_GN))
            if t >= 2:
                slot_order.append((2 * TILES + t - 2, EPS1))
        turn_of = {slot: n for n, (slot, _) in enumerate(slot_order)}

        def destination(kind, h, c):
            if kind == "Q":
                return QT[:, h % 2, c * 512:(c + 1) * 512]
            if kind == "K":
                return KT[:, h % 2, c * 512:(c + 1) * 512]
            if kind == "V":
                return V[:, h % 2, :, 2 * c:2 * c + 2, :].rearrange("p t b e -> p b t e")
            return O[:, c // 2, 4 * (c % 2):4 * (c % 2) + 4, h, :]

        def source(kind, bank):
            if kind == "V":
                return bank[:, :].rearrange("p (b t e) -> p b t e", b=2, t=2)
            if kind == "O":
                return bank[:, :].rearrange("p (b e) -> p b e", b=4)
            return bank[:, :]

        @block.sync
        def _(sp):
            sp.dma_start(ident[:, :], io["ident"]).then_inc(ident_in, 16)
            for q in range(4):
                sp.dma_start(x[:, 4 * q:4 * q + 4, :],
                             io["x"][512 * q:512 * q + 512, :].rearrange("(t p) d -> p t d", p=P)
                             ).then_inc(x_in[q], 16)
            sp.dma_start(wh[:, :, :], io["wh"].rearrange("h d e -> d h e")).then_inc(wh_in, 16)
            for h in range(2):
                sp.dma_start(ctxT[:, h, :], io["ctxT"][h * P:(h + 1) * P, :]).then_inc(ctx_in[h], 16)
            sp.dma_start(mask[:, :, :, :], io["mask"]).then_inc(mask_in, 16)
            sp.dma_start(wg[:, :, :], io["wg"].rearrange("(k p) n -> p k n", p=P)).then_inc(wg_in, 16)
            sp.dma_start(wo[:, :, :], io["wo"].rearrange("(k p) n -> p k n", p=P)).then_inc(wo_in, 16)
            sp.dma_start(wr[:, :, :], io["wrT"].rearrange("(k p) n -> p k n", p=P)).then_inc(wr_in, 16)
            sp.dma_start(gamma[:, :], io["gamma"].to_broadcast([P, D])).then_inc(gb_in, 16)
            sp.dma_start(beta[:, :], io["beta"].to_broadcast([P, D])).then_inc(gb_in, 16)
            sp.wait_ge(pad_zero, 1)
            for q in range(ROUTED // 3):
                sp.dma_start(io["slots"][3 * P * q:3 * P * (q + 1), :].rearrange("(t p) d -> p t d", p=P),
                             zeros.unsqueeze(1).to_broadcast([P, 3, D])).then_inc(pads_set, 16)
            for h in range(2, HEADS):
                sp.wait_ge(fill_done, fill_of[("V", h - 2, 3)] + 1)
                sp.dma_start(ctxT[:, h % 2, :], io["ctxT"][h * P:(h + 1) * P, :]).then_inc(ctx_in[h], 16)
            for i in range(TILES):
                sp.wait_ge(xn2_ready, i + 1)
                sp.dma_start(io["xn2"][i * P:(i + 1) * P, :], xn[:, i % 2, :]).then_inc(xn2_out[i % 2], 16)
            sp.wait_ge(xn2_out[0], 16 * TILES // 2)
            sp.wait_ge(xn2_out[1], 16 * TILES // 2)

        @block.gpsimd
        def _(pool):
            nc.gpsimd.memset(zeros, 0.0).then_inc(pad_zero, 1)
            nc.gpsimd.memset(neg_half[:, :], -0.5).then_inc(half_set, 1)
            pool.wait_ge(half_set, 1)
            for n, (slot, eps) in enumerate(slot_order):
                pool.wait_ge(mv_ready, n + 1)
                nc.gpsimd.tensor_scalar(var_eps[:, slot:slot + 1], mv[:, slot, 1:2], eps, None,
                                        ALU.add).then_inc(var_ready, 1)
                pool.wait_ge(var_ready, n + 1)
                nc.gpsimd.tensor_tensor(rstd[:, slot:slot + 1], var_eps[:, slot:slot + 1], neg_half[:, :],
                                        ALU.pow).then_inc(rstd_ready, 1)

        @block.scalar
        def _(act):
            act.dma_start(keep["gates"][:, 0:1], io["g_xattn"].to_broadcast([P, 1])).then_inc(gate_in, 16)
            act.dma_start(keep["gates"][:, 1:2], io["g_ffn"].to_broadcast([P, 1])).then_inc(gate_in, 16)
            act.wait_ge(gate_in, 32)
            nc.scalar.activation(keep["tanh"][:, :], keep["gates"][:, :], ACT.Tanh).then_inc(gates_ready, 1)
            for i in range(TILES):
                act.wait_ge(xn_turned, i + 1)
                nc.scalar.activation(xnT[:, :, i * P:(i + 1) * P],
                                     (T0, T1)[i % 2][:, :].rearrange("p (k n) -> p k n", k=KD),
                                     ACT.Copy).then_inc(xnT_ready, 1)
            for item in plan:
                r = fill_of.get(item)
                if r is not None and r % 2 == 0:
                    if item == ("O", 0, 0):
                        act.wait_ge(pads_set, 16 * ROUTED // 3)
                    act.wait_ge(fill_done, r + 1)
                    nc.scalar.activation(destination(*item), source(item[0], ring[r % 4]),
                                         ACT.Copy).then_inc(act_evac, 1)
            for t in range(TILES + 5):
                i = t - 1
                if 0 <= i < TILES:
                    act.wait_ge(z_turned, i + 1)
                    if i >= 2:
                        act.wait_ge(wo_done, i - 1)
                    nc.scalar.activation(ZT[:, i % 2, :, :], (T0, T1)[i % 2][:, :].rearrange("p (k n) -> p k n", k=KD),
                                         ACT.Copy).then_inc(zT_ready, 1)
                i = t - 4
                if 0 <= i < TILES:
                    act.wait_ge(xn2_turned, i + 1)
                    if i >= 2:
                        act.wait_ge(logits_done, i - 1)
                    nc.scalar.activation(xn2T[:, i % 2, :, :], P2[:, :].rearrange("p (k n) -> p k n", k=KD),
                                         ACT.Copy).then_inc(xn2T_ready, 1)

        @block.tensor
        def _(pe):
            pe.wait_ge(ident_in, 16)
            for i in range(TILES):
                pe.wait_ge(xn_ready, i + 1)
                if i >= 2:
                    pe.wait_ge(xnT_ready, i - 1)
                for k in range(KD):
                    last = nc.tensor.transpose((T0, T1)[i % 2][:, k * P:(k + 1) * P],
                                               xn[:, i % 2, k * P:(k + 1) * P], ident[:, :])
                last.then_inc(xn_turned, 1)
            pe.wait_ge(wh_in, 16)
            pe.wait_ge(xnT_ready, TILES)
            for kind, h, c in plan:
                if kind == "S":
                    pe.wait_ge(act_evac, (fill_of[("V", h, 3)] + 1) // 2)
                    pe.wait_ge(dve_evac, (fill_of[("V", h, 3)] + 1) // 2)
                    if h:
                        pe.wait_ge(at_ready, 2 * h)
                    for tc in range(2):
                        for b in range(B):
                            last = nc.tensor.matmul((S0, S1)[tc][:, 0:S],
                                                    KT[:, h % 2, b * S + tc * P:b * S + tc * P + P],
                                                    QT[:, h % 2, b * S:(b + 1) * S],
                                                    start=(b == 0), stop=(b == B - 1))
                        last.then_inc(s_done, 1)
                    continue
                r = fill_of[(kind, h, c)]
                if r >= 4:
                    pe.wait_ge((act_evac, dve_evac)[r % 2], (r - 4) // 2 + 1)
                bank = ring[r % 4]
                if kind == "Q":
                    last = nc.tensor.matmul(bank[:, :], wh[:, h, :], xnT[:, h, c * 512:(c + 1) * 512],
                                            start=True, stop=True)
                elif kind == "K":
                    pe.wait_ge(ctx_in[h], 16)
                    last = nc.tensor.matmul(bank[:, :], wh[:, h, :], ctxT[:, h % 2, c * 512:(c + 1) * 512],
                                            start=True, stop=True)
                elif kind == "V":
                    for q in range(4):
                        n0 = (4 * c + q) * P
                        last = nc.tensor.matmul(bank[:, q * P:(q + 1) * P], ctxT[:, h % 2, n0:n0 + P],
                                                wh[:, h, :], start=True, stop=True)
                else:
                    pe.wait_ge(at_ready, 2 * h + 2)
                    sc, bg = c // 2, c % 2
                    for tc in range(2):
                        last = nc.tensor.matmul(bank[:, :], AT[:, h % 2, tc, sc * P:(sc + 1) * P],
                                                V[:, h % 2, tc, 4 * bg:4 * bg + 4, :],
                                                start=(tc == 0), stop=(tc == 1))
                last.then_inc(fill_done, 1)
            pe.wait_ge(act_evac, r // 2 + 1)
            pe.wait_ge(dve_evac, r // 2 + 1)
            for t in range(TILES + 5):
                i = t
                if i < TILES:
                    if i == 0:
                        pe.wait_ge(wg_in, 16)
                    if i >= 2:
                        pe.wait_ge(z_ready, i - 1)
                    for k in range(KD):
                        last = nc.tensor.matmul((P0, P1)[i % 2][:, :], xnT[:, k, i * P:(i + 1) * P], wg[:, k, :],
                                                start=(k == 0), stop=(k == KD - 1))
                    last.then_inc(w_done, 1)
                i = t - 1
                if 0 <= i < TILES:
                    pe.wait_ge(z_ready, i + 1)
                    if i >= 2:
                        pe.wait_ge(zT_ready, i - 1)
                    for k in range(KD):
                        last = nc.tensor.transpose((T0, T1)[i % 2][:, k * P:(k + 1) * P],
                                                   Z[:, i % 2, k * P:(k + 1) * P], ident[:, :])
                    last.then_inc(z_turned, 1)
                i = t - 2
                if 0 <= i < TILES:
                    if i == 0:
                        pe.wait_ge(wo_in, 16)
                        pe.wait_ge(at_ready, 2 * HEADS)
                    pe.wait_ge(zT_ready, i + 1)
                    if i >= 2:
                        pe.wait_ge(mv_ready, turn_of[2 * TILES + i - 2] + 1)
                    for k in range(KD):
                        last = nc.tensor.matmul((S0, S1)[i % 2][:, :], ZT[:, i % 2, k, :], wo[:, k, :],
                                                start=(k == 0), stop=(k == KD - 1))
                    last.then_inc(wo_done, 1)
                i = t - 4
                if 0 <= i < TILES:
                    pe.wait_ge(xn2_ready, i + 1)
                    if i >= 1:
                        pe.wait_ge(xn2T_ready, i)
                    for k in range(KD):
                        last = nc.tensor.transpose(P2[:, k * P:(k + 1) * P], xn[:, i % 2, k * P:(k + 1) * P],
                                                   ident[:, :])
                    last.then_inc(xn2_turned, 1)
                i = t - 5
                if 0 <= i < TILES:
                    if i == 0:
                        pe.wait_ge(wr_in, 16)
                    pe.wait_ge(xn2T_ready, i + 1)
                    for k in range(KD):
                        last = nc.tensor.matmul(P3[:, i * E:(i + 1) * E], xn2T[:, i % 2, k, :], wr[:, k, :],
                                                start=(k == 0), stop=(k == KD - 1))
                    last.then_inc(logits_done, 1)

        @block.vector
        def _(dve):
            count = [0]

            def link(ins):
                count[0] += 1
                ins.then_inc(dve_step, 1)
                dve.wait_ge(dve_step, count[0])

            def moments(src, slot):
                link(nc.vector.bn_stats(stats[:, slot, :], src))
                nc.vector.bn_aggr(mv[:, slot, :], stats[:, slot, :]).then_inc(mv_ready, 1)

            def normalised(out, src, slot):
                dve.wait_ge(mv_ready, turn_of[slot] + 1)
                dve.wait_ge(rstd_ready, turn_of[slot] + 1)
                return nc.vector.tensor_scalar(out, src, mv[:, slot, 0:1], rstd[:, slot:slot + 1],
                                               ALU.subtract, ALU.mult)

            for t in range(TILES + 2):
                if t < TILES:
                    if t % 4 == 0:
                        dve.wait_ge(x_in[t // 4], 16)
                    moments(x[:, t, :], t)
                i = t - 2
                if i >= 0:
                    if i >= 2:
                        dve.wait_ge(xn_turned, i - 1)
                    normalised(xn[:, i % 2, :], x[:, i, :], i).then_inc(xn_ready, 1)
            dve.wait_ge(mask_in, 16)
            for item in plan:
                if item[0] == "S":
                    h = item[1]
                    for tc in range(2):
                        if h or tc:
                            dve.wait_ge(at_ready, 2 * h + tc)
                        dve.wait_ge(s_done, 2 * h + tc + 1)
                        link(nc.vector.tensor_tensor(masked[:, :], (S0, S1)[tc][:, 0:S], mask[:, h, tc, :], ALU.mult))
                        link(nc.vector.tensor_scalar(AT[:, h % 2, tc, :], masked[:, :], -1.0, 1.0, ALU.mult, ALU.max))
                        nc.vector.tensor_tensor(AT[:, h % 2, tc, :], AT[:, h % 2, tc, :], masked[:, :],
                                                ALU.max).then_inc(at_ready, 1)
                    continue
                r = fill_of[item]
                if r % 2:
                    if item == ("O", 0, 1):
                        dve.wait_ge(pads_set, 16 * ROUTED // 3)
                    dve.wait_ge(fill_done, r + 1)
                    nc.vector.tensor_copy(destination(*item), source(item[0], ring[r % 4])).then_inc(dve_evac, 1)
            dve.wait_ge(act_evac, (len(fill_of) + 1) // 2)
            dve.wait_ge(dve_evac, len(fill_of) // 2)
            dve.wait_ge(gb_in, 32)
            dve.wait_ge(gates_ready, 1)

            def o_rows(i):
                return O[:, i % 2, i // 2, :, :].rearrange("p h e -> p (h e)")

            moments(o_rows(0), TILES)
            moments(o_rows(1), TILES + 1)
            for t in range(TILES + 3):
                if t + 2 < TILES:
                    moments(o_rows(t + 2), TILES + t + 2)
                i = t
                if i < TILES:
                    if i:
                        dve.wait_ge(z_ready, i)
                    link(normalised(Y, o_rows(i), TILES + i))
                    link(nc.vector.tensor_tensor(Y, Y, gamma[:, :], ALU.mult))
                    link(nc.vector.tensor_tensor(Y, Y, beta[:, :], ALU.add))
                    dve.wait_ge(w_done, i + 1)
                    if i >= 2:
                        dve.wait_ge(z_turned, i - 1)
                    nc.vector.scalar_tensor_tensor(Z[:, i % 2, :], (P0, P1)[i % 2][:, :], 0.0, Y,
                                                   ALU.max, ALU.mult).then_inc(z_ready, 1)
                i = t - 2
                if 0 <= i < TILES:
                    dve.wait_ge(wo_done, i + 1)
                    link(nc.vector.scalar_tensor_tensor(x[:, i, :], (S0, S1)[i % 2][:, :], keep["tanh"][:, 0:1],
                                                        x[:, i, :], ALU.mult, ALU.add))
                    moments(x[:, i, :], 2 * TILES + i)
                i = t - 3
                if 0 <= i < TILES:
                    if i >= 2:
                        dve.wait_ge(xn2_turned, i - 1)
                        dve.wait_ge(xn2_out[i % 2], 16 * (i // 2))
                    normalised(xn[:, i % 2, :], x[:, i, :], 2 * TILES + i).then_inc(xn2_ready, 1)

            dve.wait_ge(logits_done, TILES)
            nc.vector.tensor_copy(keep["logits"][:, :], P3[:, 0:TILES * E]).then_inc(dve_step, 1)


UP_SPANS = [(0, 228), (228, 227), (455, 227)]
UP_COLS = 2 * HID
DOWN_AT = KD * UP_COLS
WIDTH = DOWN_AT + (HC + 1) * D
UP_PIECES = [(c, min(D, DOWN_AT - c), P) for c in range(0, DOWN_AT, D)]
PIECES = UP_PIECES + [(DOWN_AT + j * D, D, P if j < HC else 3 * HT) for j in range(HC + 1)]
UP_NEEDS = [-(-KD * 2 * (h0 + n) // D) for h0, n in UP_SPANS]
NP, NU = len(PIECES), len(UP_PIECES)
RING = 4
POOL_FIRST = 8
TURNS = {s: range(POOL_FIRST + 3 * (s - 3), POOL_FIRST + 3 * (s - 2)) for s in (3, 4, 5)}
OTHERS = NP - POOL_FIRST
FIRST_UPS = (UP_NEEDS[1] + 1, NP - 2, NP)
ORDER = [E] + list(range(E)) + [E]
PARTS = ((1, 0), (0, 1), (0, 0))


def route_and_feed_forward(nc, io, keep, banks):
    ctx = ExitStack()
    with ctx:
        def sb(name, shape, dt=F32):
            return ctx.enter_context(nc.sbuf_tensor(name, shape, dt))

        def sem(name):
            return ctx.enter_context(nc.semaphore(name))

        ident = keep["ident"]
        ring = sb("ring", [P, RING, D])
        rows = sb("rows", [P, 4, D])
        w = [sb(f"w_{x}", [P, 2, WIDTH], F32R) for x in ("hi", "lo")]
        xg = sb("xg", [P, D])
        xT = [sb(f"xT_{x}", [P, KD, P], F32R) for x in ("hi", "lo")]
        hid = sb("hid", [P, HID])
        tail = sb("tail", [P, P], F32R)
        hT = [sb("hT_hi", [P, HC + 1, P], F32R), sb("hT_lo", [P, HC, P], F32R)]
        out_sb = sb("out_sb", [P, D])
        lt = sb("lt", [P, 5, TILES * E])
        tri = sb("tri", [P, 2, P])
        thr = out_sb[:, 0:ROUTED * (E - 1)]
        small = sb("small", [P, 5, TILES])
        cst = sb("cst", [P, E + E * THR + ROUTED + 1])
        lo_rows = cst[0:3 * HT, E + E * THR + ROUTED:]
        ends = sb("ends", [P, 2, E])
        expert = sb("expert", [P, ROUTED])
        gate_of = sb("gate_of", [P, 2, TILES])
        slot = sb("slot", [P, 2 * TILES], I32)
        parity = sb("parity", [P, ROUTED], I32)
        needs = sb("needs", [P, 2, ROUTED], I32)
        free_at = sb("free_at", [P, 2, E - 1], I32)

        up_bank, hturn_bank, xturn_bank, down_bank, rank_bank = banks[0:3], banks[3:5], banks[5], banks[6], banks[7]

        ring_in = [sem(f"ring_in{q}") for q in range(RING)]
        buffer_free = sem("buffer_free")
        zeroed, hi_other, split_other, hi_split, split = sem("zeroed"), sem("hi_other"), sem("split_other"), sem("hi_split"), sem("split")
        tail_hi, tail_ready, masked = sem("tail_hi"), sem("tail_ready"), sem("masked")
        x_in, x_turned, x_hi, x_lo = sem("x_in"), sem("x_turned"), sem("x_hi"), sem("x_lo")
        up_done, silu_done, h_done = sem("up_done"), sem("silu_done"), sem("h_done")
        h_turned, h_hi, h_lo = sem("h_turned"), sem("h_hi"), sem("h_lo")
        down_done, down_taken, out_ready, stored = sem("down_done"), sem("down_taken"), sem("out_ready"), sem("stored")
        cst_in, dve_step, shifted, exped, chosen, ranked = (sem("cst_in"), sem("dve_step"), sem("shifted"),
                                                           sem("exped"), sem("chosen"), sem("ranked"))
        slots_ready, tables_ready = sem("slots_ready"), sem("tables_ready")
        tile_in = [sem(f"tile_in{q}") for q in range(4)]
        tile_out = [sem(f"tile_out{q}") for q in range(4)]
        row_in = [sem(f"row_in{q}") for q in range(4)]
        row_added, y_out = sem("row_added"), sem("y_out")
        block = ctx.enter_context(nc.Block())

        shared_tile = list(range(FIRST)) + [None] * ROUTED + list(range(FIRST, TILES))

        def pair(i):
            return (rows, ring)[i % 4 // 2][:, 2 * (i % 2):2 * (i % 2) + 2, :]

        def part(q, buf, piece):
            c0, n, rows_ = PIECES[piece]
            if piece == NP - 1:
                q = 1 - q
            return w[q][0:rows_, buf, c0:c0 + n]

        def added_in(m):
            return range((m - 2) * TILES // (LAST - 2), (m - 1) * TILES // (LAST - 2)) if 2 <= m < LAST else range(0)

        def complete_at(i):
            return max(i - FIRST + 1, next(m for m in range(1, LAST + 1) if i in added_in(m)))

        @block.sync
        def _(sp):
            def load(version, piece):
                n = version * NP + piece
                m = n - RING
                if NP <= m < NP + POOL_FIRST:
                    sp.wait_ge(split, m - NP + 1)
                elif m >= 2 * NP:
                    sp.wait_ge(split, m - NP - OTHERS + 1)
                elif m >= 0:
                    sp.wait_ge(split_other, m + 1 if m < NP else m + 1 - POOL_FIRST)
                e, (c0, cols, rows_) = ORDER[version], PIECES[piece]
                if c0 < DOWN_AT:
                    src = io["w_up"][e, :, c0:c0 + cols]
                elif rows_ == P:
                    src = io["w_down"][e, :, (c0 - DOWN_AT) // D, :]
                else:
                    src = io["w_downt"][e, :, :]
                sp.dma_start(ring[0:rows_, n % RING, 0:cols], src).then_inc(ring_in[n % RING], 16)

            def load_tile(i):
                if i >= 4:
                    sp.wait_ge(tile_out[i % 4], 32 * (i // 4))
                sp.dma_start(rows[:, i % 4, :], io["xn2"][i * P:(i + 1) * P, :]).then_inc(tile_in[i % 4], 16)

            for piece in range(NP):
                if piece == RING:
                    sp.dma_start(tri[:, :, :], io["tri"]).then_inc(cst_in, 16)
                    sp.dma_start(cst[:, :], io["cst"]).then_inc(cst_in, 16)
                load(0, piece)
            for i in range(4):
                load_tile(i)
            for piece in range(POOL_FIRST):
                load(1, piece)
            for i in range(4, TILES):
                load_tile(i)
                if POOL_FIRST + i - 4 < NP:
                    load(1, POOL_FIRST + i - 4)
            for version in range(2, len(ORDER)):
                for piece in range(NP):
                    load(version, piece)

        @block.gpsimd
        def _(pool):
            def split_pieces(version, first, end):
                for piece in range(first, end + 1):
                    if piece < end:
                        n = version * NP + piece
                        c0, cols, rows_ = PIECES[piece]
                        pool.wait_ge(ring_in[n % RING], 16 * (n // RING + 1))
                        nc.gpsimd.tensor_copy(part(0, version % 2, piece),
                                              ring[0:rows_, n % RING, 0:cols]).then_inc(hi_split, 1)
                    if piece > first:
                        n = version * NP + piece - 1
                        c0, cols, rows_ = PIECES[piece - 1]
                        pool.wait_ge(hi_split, n + 1 - NP - (OTHERS if version > 1 else 0))
                        if piece == NP:
                            nc.gpsimd.tensor_scalar(ring[0:rows_, n % RING, 0:cols], ring[0:rows_, n % RING, 0:cols],
                                                    lo_rows, None, ALU.mult).then_inc(masked, 1)
                            pool.wait_ge(masked, version - 1)
                        nc.gpsimd.tensor_tensor(part(1, version % 2, piece - 1), ring[0:rows_, n % RING, 0:cols],
                                                part(0, version % 2, piece - 1).bitcast(F32),
                                                ALU.subtract).then_inc(split, 1)

            pool.wait_ge(cst_in, 32)
            split_pieces(1, 0, POOL_FIRST)
            pool.wait_ge(slots_ready, 2)
            for i in range(TILES):
                pool.wait_ge(tile_in[i % 4], 16 * (i // 4 + 1))
                for c in range(2):
                    nc.gpsimd.indirect_dma_start(
                        out=io["slots"], out_offset=bass.IndirectOffsetOnAxis(slot[:, c * TILES + i:c * TILES + i + 1], 0),
                        in_=rows[:, i % 4, :], in_offset=None).then_inc(tile_out[i % 4], 16)
            pool.wait_ge(up_done, 3 * FIRST)
            split_pieces(2, 0, NU)
            pool.wait_ge(down_done, FIRST)
            split_pieces(2, NU, NP)
            pool.wait_ge(tables_ready, 3)
            for version in range(3, len(ORDER)):
                for q, (done, lowest, first, end) in enumerate(((up_done, 3, 0, NU), (down_done, 1, NU, NP))):
                    at = pool.value_load(free_at[0:1, q, version - 3:version - 2], min_val=lowest * (FIRST + 1),
                                         max_val=lowest * (FIRST + ROUTED))
                    pool.wait_ge(done, at)
                    pool.sem_inc(buffer_free, 1)
                    pool.wait_ge(buffer_free, 2 * (version - 3) + q + 1)
                    split_pieces(version, first, end)
            for q in range(4):
                pool.wait_ge(tile_out[q], 32 * TILES // 4)
            pool.wait_ge(split, NP * (len(ORDER) - 1) - OTHERS)
            pool.wait_ge(stored, 16 * ROUTED)
            for i in range(TILES):
                if i >= 4:
                    pool.wait_ge(row_added, 2 * (i - 3))
                for c in range(2):
                    nc.gpsimd.indirect_dma_start(
                        out=pair(i)[:, c, :], out_offset=None, in_=io["routed"],
                        in_offset=bass.IndirectOffsetOnAxis(slot[:, c * TILES + i:c * TILES + i + 1], 0)
                    ).then_inc(row_in[i % 4], 16)

        @block.scalar
        def _(act):
            def load_x(s, loop=None):
                if loop is not None:
                    act.dma_start(xg[:, :], io["slots"][bass.ds(loop * P, P), :]).then_inc(x_in, 16)
                    return
                if s >= STEPS:
                    return
                if s == FIRST:
                    for q in range(4):
                        act.wait_ge(tile_out[q], 32 * TILES // 4)
                i = shared_tile[s]
                src = io["slots"][(s - FIRST) * P:(s - FIRST + 1) * P, :] if i is None else io["xn2"][i * P:(i + 1) * P, :]
                act.dma_start(xg[:, :], src).then_inc(x_in, 16)

            def high(version, piece):
                n = version * NP + piece
                c0, cols, rows_ = PIECES[piece]
                act.wait_ge(ring_in[n % RING], 16 * (n // RING + 1))
                nc.scalar.activation(part(0, version, piece), ring[0:rows_, n % RING, 0:cols], ACT.Copy).then_inc(hi_other, 1)

            def tail_high(s):
                act.wait_ge(h_done, 3 * s + 3)
                nc.scalar.activation(tail[:, HT:2 * HT], hid[:, HC * P:HID], ACT.Copy).then_inc(tail_hi, 1)
                nc.scalar.activation(tail[:, 2 * HT:3 * HT], hid[:, HC * P:HID], ACT.Copy,
                                     scale=-1.0).then_inc(tail_hi, 1)

            def x_high(s):
                act.wait_ge(x_turned, s + 1)
                nc.scalar.activation(xT[0][:, :, :], xturn_bank[:, :].rearrange("p (k n) -> p k n", k=KD),
                                     ACT.Copy).then_inc(x_hi, 1)

            def h_high(s):
                for q, (a, b) in enumerate(((0, 4), (4, 6))):
                    act.wait_ge(h_turned, 2 * s + q + 1)
                    nc.scalar.activation(hT[0][:, a:b, :], hturn_bank[q][:, 0:(b - a) * P].rearrange("p (k n) -> p k n", k=b - a),
                                         ACT.Copy).then_inc(h_hi, 1)

            def iteration(s, up=True, turn=True, down=True, routed_down=False, loop=None):
                for c in range(3):
                    if up:
                        if c == 0 and down:
                            act.wait_ge(h_turned, 2 * s)
                        silu(s, c)
                    if c == 0 and down:
                        h_high(s - 1)
                if up:
                    tail_high(s)
                if turn:
                    x_high(s + 1)
                    load_x(s + 2, None if loop is None else loop + 2)
                if down and routed_down:
                    act.wait_ge(down_done, s)
                    m = s - FIRST
                    if loop is not None or m > 1:
                        act.wait_ge(stored, 16 * (m - 1))
                    nc.scalar.activation(out_sb[:, :], down_bank[:, :], ACT.Copy).then_inc(out_ready, 1)
                    act.wait_ge(out_ready, m + 1)
                    dst = io["routed"][(m - 1) * P:m * P, :] if loop is None else io["routed"][bass.ds((loop - 1) * P, P), :]
                    act.dma_start(dst, out_sb[:, :]).then_inc(stored, 16)

            load_x(0)
            act.wait_ge(shifted, 1)
            nc.scalar.activation(lt[:, 1, :], lt[:, 0, :], ACT.Exp).then_inc(exped, 1)
            def silu(s, c):
                h0, n = UP_SPANS[c]
                act.wait_ge(up_done, 3 * s + c + 1)
                nc.scalar.activation(hid[:, h0:h0 + n], up_bank[c][:, 0:n], ACT.Silu).then_inc(silu_done, 1)

            for piece in range(NP):
                high(0, piece)
                if piece + 1 == UP_NEEDS[0]:
                    x_high(0)
                    load_x(1)
                if piece + 1 in FIRST_UPS:
                    silu(0, FIRST_UPS.index(piece + 1))
            tail_high(0)
            x_high(1)
            load_x(2)
            for s in range(1, FIRST + 2):
                if s == FIRST + 1:
                    act.wait_ge(down_taken, FIRST)
                    act.wait_ge(tables_ready, 3)
                    act.sem_inc(out_ready, 1)
                iteration(s, routed_down=s > FIRST)
                for piece in TURNS.get(s, ()):
                    high(1, piece)
            with act.Fori(2, ROUTED - 2) as r:
                iteration(r + FIRST, routed_down=True, loop=r)
            for s in range(FIRST + ROUTED - 2, STEPS + 1):
                iteration(s, up=s < STEPS, turn=s + 1 < STEPS, routed_down=s <= FIRST + ROUTED)
                m = s - FIRST - ROUTED
                for i in range(TILES):
                    if m > 0 and complete_at(i) == m:
                        act.wait_ge(down_taken, FIRST + m)
                        act.wait_ge(row_added, 2 * i + 2)
                        act.dma_start(io["out"][i * P:(i + 1) * P, :], keep["x"][:, i, :]).then_inc(y_out, 16)
            act.wait_ge(y_out, 16 * TILES)

        @block.tensor
        def _(pe):
            def turn_x(s):
                pe.wait_ge(x_in, 16 * (s + 1))
                if not isinstance(s, int) or s:
                    pe.wait_ge(x_lo, s)
                for k in range(KD):
                    mm = nc.tensor.transpose(xturn_bank[:, k * P:(k + 1) * P], xg[:, k * P:(k + 1) * P], ident[:, :])
                mm.then_inc(x_turned, 1)

            def moving(q, buf, c0, n, rows_=P):
                if isinstance(buf, int):
                    return w[q][0:rows_, buf, c0:c0 + n]
                return w[q][0:rows_, bass.ds(buf, 1), c0:c0 + n].rearrange("p o n -> p (o n)")

            def up(s, c, buf):
                c0 = KD * 2 * UP_SPANS[c][0]
                n = 2 * UP_SPANS[c][1]
                if not isinstance(s, int) or s:
                    pe.wait_ge(h_done, 3 * s + c - 2)
                for g, (a, b) in enumerate(PARTS):
                    for k in range(KD):
                        mm = nc.tensor.matmul(up_bank[c][:, 0:n], xT[a][:, k, :], moving(b, buf, c0 + k * n, n),
                                              start=(g == 0 and k == 0), stop=(g == 2 and k == KD - 1))
                mm.then_inc(up_done, 1)

            def turn_h(s):
                pe.wait_ge(h_done, 3 * s + 3)
                pe.wait_ge(tail_ready, s + 1)
                if not isinstance(s, int) or s:
                    pe.wait_ge(h_lo, 2 * s)
                for j in range(HC + 1):
                    src = hid[:, j * P:(j + 1) * P] if j < HC else tail[:, :].bitcast(F32)
                    mm = nc.tensor.transpose(hturn_bank[j // 4][:, (j % 4) * P:(j % 4 + 1) * P], src, ident[:, :])
                    if j in (3, HC):
                        mm.then_inc(h_turned, 1)

            def down(s, buf, taken, n_taken):
                pe.wait_ge(h_lo, 2 * s + 2)
                if taken is not None:
                    pe.wait_ge(taken, n_taken)
                for j in range(HC):
                    for g, (a, b) in enumerate(PARTS):
                        nc.tensor.matmul(down_bank[:, :], hT[a][:, j, :], moving(b, buf, DOWN_AT + j * D, D),
                                         start=(j == 0 and g == 0), stop=False)
                mm = nc.tensor.matmul(down_bank[:, :], hT[0][0:3 * HT, HC, :],
                                      moving(0, buf, DOWN_AT + HC * D, D, 3 * HT), start=False, stop=True)
                mm.then_inc(down_done, 1)

            turn_x(0)
            for s in range(FIRST + 1):
                pe.wait_ge(x_lo, s + 1)
                if s == FIRST:
                    pe.wait_ge(split, POOL_FIRST)
                    pe.wait_ge(split_other, NP + NU - POOL_FIRST)
                buf = s // FIRST
                for c in range(3):
                    if s == 0:
                        pe.wait_ge(split_other, UP_NEEDS[c])
                    up(s, c, buf)
                    if s and c == 0:
                        turn_h(s - 1)
                if s == 1:
                    pe.wait_ge(split_other, NP)
                    pe.wait_ge(cst_in, 32)
                    pe.wait_ge(chosen, 1)
                    nc.tensor.matmul(rank_bank[:, 0:TILES * E], tri[:, 0, :], lt[:, 4, :], start=True, stop=True)
                    nc.tensor.matmul(rank_bank[:, TILES * E:2 * TILES * E], tri[:, 1, :], lt[:, 4, :], start=True,
                                     stop=True).then_inc(ranked, 1)
                turn_x(s + 1)
                if s:
                    down(s - 1, 0, down_taken if s > 1 else None, s - 1)
            pe.wait_ge(split_other, NP + OTHERS)
            pe.wait_ge(tables_ready, 3)
            with pe.Fori(1, ROUTED - 1) as r:
                buf = pe.value_load(parity[0:1, bass.ds(r, 1)], min_val=0, max_val=1)
                buf_before = pe.value_load(parity[0:1, bass.ds(r - 1, 1)], min_val=0, max_val=1)
                need_up = pe.value_load(needs[0:1, 0, bass.ds(r, 1)], min_val=NU - OTHERS, max_val=NP * E)
                need_down = pe.value_load(needs[0:1, 1, bass.ds(r - 1, 1)], min_val=NP - OTHERS, max_val=NP * E)
                s = r + FIRST
                pe.wait_ge(split, need_up)
                pe.wait_ge(x_lo, s + 1)
                up(s, 0, buf)
                turn_h(s - 1)
                up(s, 1, buf)
                up(s, 2, buf)
                turn_x(s + 1)
                pe.wait_ge(split, need_down)
                down(s - 1, buf_before, out_ready, r)
            for s in range(FIRST + ROUTED - 1, STEPS + 1):
                m = s - FIRST - ROUTED
                if s < STEPS:
                    pe.wait_ge(x_lo, s + 1)
                    buf = 0 if m < 0 else 1
                    pe.wait_ge(split, NP * (E - 1 + (m >= 0)) + NU - OTHERS)
                    up(s, 0, buf)
                turn_h(s - 1)
                if s < STEPS:
                    up(s, 1, buf)
                    up(s, 2, buf)
                if s + 1 < STEPS:
                    turn_x(s + 1)
                if m == -1:
                    before = pe.value_load(parity[0:1, ROUTED - 2:ROUTED - 1], min_val=0, max_val=1)
                    need_down = pe.value_load(needs[0:1, 1, ROUTED - 2:ROUTED - 1], min_val=NP - OTHERS, max_val=NP * E)
                    pe.wait_ge(split, need_down)
                    down(s - 1, before, out_ready, s - FIRST)
                elif m <= 1:
                    pe.wait_ge(split, NP * (E + m) - OTHERS)
                    down(s - 1, m, out_ready, s - FIRST)
                else:
                    down(s - 1, 1, down_taken, FIRST + m - 1)

        @block.vector
        def _(dve):
            count = [0]

            def link(ins):
                count[0] += 1
                ins.then_inc(dve_step, 1)
                dve.wait_ge(dve_step, count[0])

            nc.vector.memset(tail[:, 3 * HT:P].bitcast(F32), 0.0).then_inc(zeroed, 1)
            dve.wait_ge(zeroed, 1)

            def low(version, piece):
                n = version * NP + piece
                c0, cols, rows_ = PIECES[piece]
                k = n if version == 0 else n - POOL_FIRST
                dve.wait_ge(hi_other, k + 1)
                whole, high = ring[0:rows_, n % RING, 0:cols], part(0, version, piece).bitcast(F32)
                if piece < NP - 1:
                    nc.vector.tensor_tensor(part(1, version, piece), whole, high, ALU.subtract).then_inc(split_other, 1)
                else:
                    dve.wait_ge(cst_in, 32)
                    nc.vector.scalar_tensor_tensor(part(1, version, piece), whole, lo_rows, high, ALU.mult,
                                                   ALU.subtract).then_inc(split_other, 1)

            def mult(s, c):
                h0, n = UP_SPANS[c]
                dve.wait_ge(silu_done, 3 * s + c + 1)
                u = hid[:, h0:h0 + n]
                nc.vector.tensor_tensor(u, u, up_bank[c][:, n:2 * n], ALU.mult).then_inc(h_done, 1)

            def tail_low(s):
                dve.wait_ge(tail_hi, 2 * s + 2)
                nc.vector.tensor_tensor(tail[:, 0:HT], tail[:, HT:2 * HT].bitcast(F32), hid[:, HC * P:HID],
                                        ALU.subtract).then_inc(tail_ready, 1)

            def x_low(s):
                dve.wait_ge(x_hi, s + 1)
                nc.vector.tensor_tensor(xT[1][:, :, :], xturn_bank[:, :].rearrange("p (k n) -> p k n", k=KD),
                                        xT[0][:, :, :].bitcast(F32), ALU.subtract).then_inc(x_lo, 1)

            def iteration(s, up=True, turn=True, down=True, add_shared=None):
                for c in range(3):
                    if up:
                        mult(s, c)
                    if c == 0 and down:
                        for q, (a, b) in enumerate(((0, 4), (4, 6))):
                            dve.wait_ge(h_hi, 2 * (s - 1) + q + 1)
                            b = min(b, HC)
                            nc.vector.tensor_tensor(hT[1][:, a:b, :],
                                                    hturn_bank[q][:, 0:(b - a) * P].rearrange("p (k n) -> p k n", k=b - a),
                                                    hT[0][:, a:b, :].bitcast(F32), ALU.subtract).then_inc(h_lo, 1)
                if up:
                    tail_low(s)
                if turn:
                    x_low(s + 1)
                if add_shared is not None:
                    i = add_shared
                    dve.wait_ge(down_done, s)
                    nc.vector.scalar_tensor_tensor(keep["x"][:, i, :], down_bank[:, :], keep["tanh"][:, 1:2],
                                                   keep["x"][:, i, :], ALU.mult, ALU.add).then_inc(down_taken, 1)

            def by_expert(n):
                return lt[:, n, :].rearrange("p (t e) -> p t e", e=E)

            def over(ap):
                return ap.unsqueeze(2).to_broadcast([P, TILES, E])

            logits = keep["logits"][:, :].rearrange("p (t e) -> p t e", e=E)
            experts = cst[:, 0:E].unsqueeze(1).to_broadcast([P, TILES, E])

            def softmax_shift():
                link(nc.vector.tensor_reduce(small[:, 0, :], logits, X, ALU.max))
                nc.vector.tensor_tensor(by_expert(0), logits, over(small[:, 0, :]), ALU.subtract).then_inc(shifted, 1)

            def choose():
                dve.wait_ge(exped, 1)
                link(nc.vector.tensor_reduce(small[:, 1, :], by_expert(1), X, ALU.add))
                link(nc.vector.reciprocal(small[:, 1, :], small[:, 1, :]))
                link(nc.vector.tensor_tensor(by_expert(1), by_expert(1), over(small[:, 1, :]), ALU.mult))
                dve.wait_ge(cst_in, 32)
                for c in range(2):
                    onehot = by_expert(2 + c)
                    link(nc.vector.tensor_reduce(small[:, 2 + c, :], by_expert(1), X, ALU.max))
                    link(nc.vector.tensor_tensor(by_expert(0), by_expert(1), over(small[:, 2 + c, :]), ALU.is_equal))
                    link(nc.vector.tensor_tensor(by_expert(0), by_expert(0), experts, ALU.mult))
                    link(nc.vector.tensor_reduce(small[:, 4, :], by_expert(0), X, ALU.min))
                    link(nc.vector.tensor_tensor(onehot, over(small[:, 4, :]), experts, ALU.is_equal))
                    if c == 0:
                        link(nc.vector.scalar_tensor_tensor(lt[:, 1, :], lt[:, 2, :], -2.0, lt[:, 1, :], ALU.mult, ALU.add))
                nc.vector.tensor_tensor(lt[:, 4, :], lt[:, 2, :], lt[:, 3, :], ALU.add).then_inc(chosen, 1)

            def weigh():
                link(nc.vector.tensor_tensor(small[:, 4, :], small[:, 2, :], small[:, 3, :], ALU.add))
                link(nc.vector.reciprocal(small[:, 4, :], small[:, 4, :]))
                link(nc.vector.tensor_scalar(small[:, 4, :], small[:, 4, :], keep["tanh"][:, 1:2], None, ALU.mult))
                for c in range(2):
                    link(nc.vector.tensor_tensor(gate_of[:, c, :], small[:, 2 + c, :], small[:, 4, :], ALU.mult))

            def place():
                dve.wait_ge(ranked, 1)
                rank, total = rank_bank[:, 0:TILES * E], rank_bank[:, TILES * E:2 * TILES * E]
                link(nc.vector.tensor_copy(lt[:, 0, :], total))
                a, b, d = 0, 1, 1
                while d < TILES:
                    link(nc.vector.tensor_copy(lt[:, b, 0:d * E], lt[:, a, 0:d * E]))
                    link(nc.vector.tensor_tensor(lt[:, b, d * E:], lt[:, a, d * E:], lt[:, a, 0:(TILES - d) * E], ALU.add))
                    a, b, d = b, a, 2 * d
                counts = lt[:, a, (TILES - 1) * E:TILES * E]
                over_thr = thr[:, 0:E * THR].rearrange("p (e k) -> p e k", k=THR)
                link(nc.vector.tensor_tensor(over_thr, counts.unsqueeze(2).to_broadcast([P, E, THR]),
                                             cst[:, E:E + E * THR].rearrange("p (e k) -> p e k", k=THR), ALU.is_gt))
                link(nc.vector.tensor_reduce(ends[:, 0, :], over_thr, X, ALU.add))
                u, v, d = 0, 1, 1
                while d < E:
                    link(nc.vector.tensor_copy(ends[:, v, 0:d], ends[:, u, 0:d]))
                    link(nc.vector.tensor_tensor(ends[:, v, d:E], ends[:, u, d:E], ends[:, u, 0:E - d], ALU.add))
                    u, v, d = v, u, 2 * d
                link(nc.vector.tensor_tensor(lt[:, 4, :], lt[:, a, :], total, ALU.subtract))
                link(nc.vector.tensor_tensor(lt[:, 4, :], lt[:, 4, :], rank, ALU.add))
                link(nc.vector.memset(ends[:, v, 0:1], 0.0))
                link(nc.vector.tensor_scalar(ends[:, v, 1:E], ends[:, u, 0:E - 1], float(P), None, ALU.mult))
                link(nc.vector.tensor_tensor(by_expert(4), by_expert(4),
                                             ends[:, v, :].unsqueeze(1).to_broadcast([P, TILES, E]), ALU.add))
                for c in range(2):
                    link(nc.vector.tensor_tensor(lt[:, 0, :], lt[:, 2 + c, :], lt[:, 4, :], ALU.mult))
                    link(nc.vector.tensor_reduce(small[:, c, :], by_expert(0), X, ALU.add))
                    nc.vector.tensor_copy(slot[:, c * TILES:(c + 1) * TILES], small[:, c, :]).then_inc(slots_ready, 1)
                return ends[:, u, 0:E - 1]

            def tables(end):
                at = thr.rearrange("p (s e) -> p s e", e=E - 1)
                link(nc.vector.tensor_tensor(at, end.unsqueeze(1).to_broadcast([P, ROUTED, E - 1]),
                                             cst[:, E + E * THR:E + E * THR + ROUTED].unsqueeze(2).to_broadcast([P, ROUTED, E - 1]), ALU.is_le))
                link(nc.vector.tensor_reduce(expert[:, :], at, X, ALU.add))
                for q, n in enumerate((NU, NP)):
                    link(nc.vector.tensor_scalar(needs[:, q, :], expert[:, :], float(NP), float(n - OTHERS), ALU.mult, ALU.add))
                link(nc.vector.tensor_scalar(expert[:, :], expert[:, :], 1.0, None, ALU.add))
                link(nc.vector.tensor_copy(parity[:, :], expert[:, :]))
                nc.vector.tensor_scalar(parity[:, :], parity[:, :], 1, None, ALU.bitwise_and).then_inc(tables_ready, 1)
                for q, n in enumerate((3.0, 1.0)):
                    nc.vector.tensor_scalar(free_at[:, q, :], end, n, n * FIRST, ALU.mult, ALU.add).then_inc(tables_ready, 1)

            softmax_shift()
            for piece in range(NP):
                low(0, piece)
                if piece + 1 == UP_NEEDS[0]:
                    x_low(0)
                if piece + 1 in FIRST_UPS:
                    mult(0, FIRST_UPS.index(piece + 1))
            tail_low(0)
            x_low(1)
            choose()
            weigh()
            for s in range(1, FIRST + 1):
                if s == 2:
                    end = place()
                if s == 3:
                    tables(end)
                iteration(s, add_shared=shared_tile[s - 1])
                for piece in TURNS.get(s, ()):
                    low(1, piece)
            with dve.Fori(1, ROUTED - 1) as r:
                iteration(r + FIRST)
            for s in range(FIRST + ROUTED - 1, STEPS + 1):
                m = s - FIRST - ROUTED
                iteration(s, up=s < STEPS, turn=s + 1 < STEPS)
                if m < 1:
                    continue
                dve.wait_ge(down_taken, FIRST + m - 1)
                for i in added_in(m):
                    dve.wait_ge(row_in[i % 4], 32 * (i // 4 + 1))
                    for c in range(2):
                        nc.vector.scalar_tensor_tensor(keep["x"][:, i, :], pair(i)[:, c, :],
                                                       gate_of[:, c, i:i + 1], keep["x"][:, i, :],
                                                       ALU.mult, ALU.add).then_inc(row_added, 1)
                        dve.wait_ge(row_added, 2 * i + c + 1)
                i = shared_tile[s - 1]
                dve.wait_ge(down_done, s)
                nc.vector.scalar_tensor_tensor(keep["x"][:, i, :], down_bank[:, :], keep["tanh"][:, 1:2],
                                               keep["x"][:, i, :], ALU.mult, ALU.add).then_inc(down_taken, 1)


def build(nc, io):
    io["xn2"] = nc.dram_tensor("xn2_rows", (N, D), F32, kind="Internal").ap()
    io["slots"] = nc.dram_tensor("slot_rows", (ROUTED * P, D), F32, kind="Internal").ap()
    io["routed"] = nc.dram_tensor("routed_rows", (ROUTED * P, D), F32, kind="Internal").ap()
    with ExitStack() as ctx:
        def sb(name, shape, dt=F32):
            return ctx.enter_context(nc.sbuf_tensor(name, shape, dt))

        keep = {
            "x": sb("x_all", [P, TILES, D]),
            "ident": sb("ident", [P, P]),
            "gates": sb("gates", [P, 2]),
            "tanh": sb("tanh_gates", [P, 2]),
            "logits": sb("logits", [P, TILES * E]),
        }
        banks = [ctx.enter_context(nc.psum_tensor(f"bank{i}", [P, 512], F32)) for i in range(8)]
        attention(nc, io, keep, banks)
        route_and_feed_forward(nc, io, keep, banks)


def decay_masks():
    gam = 1.0 - 2.0 ** (-5.0 - np.arange(HEADS, dtype=np.float64))
    idx = np.arange(S, dtype=np.float64)
    expo = idx[None, :] - idx[:, None]
    d = np.where(expo[None] <= 0, gam[:, None, None] ** np.minimum(expo, 0)[None], 0.0)
    d = d / np.sqrt(d.sum(-1))[:, None, :] / np.sqrt(float(HD))
    return d.transpose(2, 0, 1).reshape(2, P, HEADS, S).transpose(1, 2, 0, 3).astype(np.float32)


def kernel(**inputs):
    import numpy as _np
    import concourse.bacc as _bacc
    from concourse.bass_utils import run_bass_kernel_spmd as _run

    a = {k: _np.asarray(v) for k, v in inputs.items()}
    w1 = _np.concatenate([a["L0_ffn_ew1"], a["L0_ffn_sw1"][None]]).transpose(0, 2, 1)
    w3 = _np.concatenate([a["L0_ffn_ew3"], a["L0_ffn_sw3"][None]]).transpose(0, 2, 1)
    w2 = _np.concatenate([a["L0_ffn_ew2"], a["L0_ffn_sw2"][None]]).transpose(0, 2, 1)
    parts = [_np.concatenate([w1[..., h0:h0 + n], w3[..., h0:h0 + n]], axis=-1).reshape(E + 1, KD, P, 2 * n)
             .transpose(0, 2, 1, 3).reshape(E + 1, P, KD * 2 * n) for h0, n in UP_SPANS]
    cut = HC * P
    limits = _np.arange(THR) * float(P)
    limits[0] = -1.0
    cst = _np.concatenate([_np.arange(E) - 8.0, _np.tile(limits, E),
                           _np.arange(ROUTED, dtype=_np.float64), _np.zeros(1)]).astype(_np.float32)
    cst = _np.tile(cst, (P, 1))
    cst[HT:2 * HT, -1] = 1.0
    arrays = {
        "x": a["x"].reshape(N, D),
        "ctxT": a["ctx_2048"].reshape(N, D).T,
        "wh": a["L0_xattn_Wh"], "wg": a["L0_xattn_wg_w"], "wo": a["L0_xattn_wo_w"],
        "gamma": a["L0_xattn_gn_gamma"].reshape(1, D), "beta": a["L0_xattn_gn_beta"].reshape(1, D),
        "wrT": a["L0_ffn_wr"].T,
        "g_xattn": a["g_xattn"].reshape(1, 1), "g_ffn": a["g_ffn"].reshape(1, 1),
        "w_up": _np.concatenate(parts, axis=-1),
        "w_down": w2[:, :cut].reshape(E + 1, HC, P, D).transpose(0, 2, 1, 3),
        "w_downt": _np.concatenate([w2[:, cut:]] * 3, axis=1),
        "ident": _np.eye(P, dtype=_np.float32),
        "tri": _np.stack([_np.triu(_np.ones((P, P)), 1), _np.ones((P, P))], axis=1).astype(_np.float32),
        "mask": decay_masks(),
        "cst": cst,
    }
    nc = _bacc.Bacc("TRN2", target_bir_lowering=False, num_devices=1)
    feed, io = {}, {}
    for name, v in arrays.items():
        v = _np.ascontiguousarray(v)
        feed[f"in_{name}"] = v
        io[name] = nc.dram_tensor(f"in_{name}", v.shape, mybir.dt.from_np(v.dtype), kind="ExternalInput").ap()
    io["out"] = nc.dram_tensor("out_y", (N, D), F32, kind="ExternalOutput").ap()
    build(nc, io)
    r = _run(nc, [feed], core_ids=[0])
    return r.results[0]["out_y"].reshape(B, S, D)
```

```python
from contextlib import ExitStack

import numpy as np

import concourse.bass as bass
from concourse import mybir

F32 = mybir.dt.float32
F32R = mybir.dt.float32r
I32 = mybir.dt.int32
ALU = mybir.AluOpType
ACT = mybir.ActivationFunctionType
X = mybir.AxisListType.X

P = 128
B, S, D = 8, 256, 512
HEADS, HD = 4, 128
N = B * S
TILES = N // P
KD = D // P
E = 8
HID = D * 4 // 3
HC = HID // P
HT = HID - HC * P
FIRST = 8
LAST = TILES - FIRST
ROUTED = (2 * N - E) // P + E
STEPS = FIRST + ROUTED + LAST
THR = N // P
EPS1, EPS_GN = 1e-5, 1e-3


UP_SPANS = [(0, 228), (228, 227), (455, 227)]
UP_COLS = 2 * HID
DOWN_AT = KD * UP_COLS
WIDTH = DOWN_AT + (HC + 1) * D
UP_PIECES = [(c, min(D, DOWN_AT - c), P) for c in range(0, DOWN_AT, D)]
PIECES = UP_PIECES + [(DOWN_AT + j * D, D, P if j < HC else 3 * HT) for j in range(HC + 1)]
UP_NEEDS = [-(-KD * 2 * (h0 + n) // D) for h0, n in UP_SPANS]
NP, NU = len(PIECES), len(UP_PIECES)
PLACES, RING = 9, 5


def place(n):
    return (n, 1) if n < PLACES else ((n - PLACES) % RING, (n - PLACES) // RING + 2)


def before(n):
    return None if n < PLACES else n - PLACES if n < PLACES + RING else n - RING


def load_piece(io, keep, sp, version, piece):
    e, (c0, cols, rows_) = ORDER[version], PIECES[piece]
    if c0 < DOWN_AT:
        src = io["w_up"][e, :, c0:c0 + cols]
    elif rows_ == P:
        src = io["w_down"][e, :, (c0 - DOWN_AT) // D, :]
    else:
        src = io["w_downt"][e, :, :]
    q = place(version * NP + piece)[0]
    sp.dma_start(keep["places"][0:rows_, q, 0:cols], src).then_inc(keep["piece_in"][q], 16)


POOL_FIRST = 8
TURNS = {s: range(POOL_FIRST + 3 * (s - 3), POOL_FIRST + 3 * (s - 2)) for s in (3, 4, 5)}
OTHERS = NP - POOL_FIRST
FIRST_UPS = (NU, NU + 2, NU + 4)
ORDER = [E] + list(range(E)) + [E]
PARTS = ((1, 0), (0, 1), (0, 0))


def attention(nc, io, keep, banks):
    ctx = ExitStack()
    with ctx:
        def sb(name, shape, dt=F32):
            return ctx.enter_context(nc.sbuf_tensor(name, shape, dt))

        def sem(name):
            return ctx.enter_context(nc.semaphore(name))

        x2 = keep["x"]
        O = x2[:, :, :].rearrange("p (b t) (h e) -> p t b h e", t=2, h=HEADS)
        w_whole = x2[:, 0:2 * KD, :]
        zeros = sb("zeros", [P, D])
        x = sb("x_ring", [P, 4, D])
        ident = keep["ident"]
        xn = sb("xn", [P, 2, D])
        xnT = [sb(f"xnT_{q}", [P, KD, N], F32R) for q in ("hi", "lo")]
        ctxT = keep["places"][:, 0:2 * N // D, :].rearrange("p (a c) d -> p a (c d)", a=2)
        wh = sb("wh", [P, HEADS, HD])
        ZT = [sb(f"ZT_{q}", [P, 2, KD, P], F32R) for q in ("hi", "lo")]
        wwT = [part[:, 0, :, :] for part in ZT]
        wgo = [sb(f"wgo_{q}", [P, 2 * KD, D], F32R) for q in ("hi", "lo")]
        wr = sb("wr", [P, KD, E])
        mask = sb("mask", [P, HEADS, 2, S])
        gamma = sb("gamma", [P, D])
        beta = sb("beta", [P, D])
        QT = sb("QT", [P, N])
        V = sb("V", [P, 2, B, HD])
        AT = sb("AT", [P, 2, 2, S])
        masked = sb("masked", [P, S])
        whT = AT[:, 1, :, :].rearrange("p a (h d) -> p (a h) d", d=HD)
        stats = sb("stats", [P, 3 * TILES, 6])
        mv = sb("mv", [P, 3 * TILES, 2])
        var_eps = sb("var_eps", [P, 3 * TILES])
        rstd = sb("rstd", [P, 3 * TILES])
        bias = sb("bias", [P, TILES, 2])
        neg_half = sb("neg_half", [P, 1])
        Y = QT[:, 0:D]
        Z = QT[:, D:3 * D].rearrange("p (a n) -> p a n", a=2)
        xn2T = V[:, 0, :, :].rearrange("p (a k) n -> p a k n", a=2)

        P0, P1, P2, P3, S0, S1, T0, T1 = banks
        ring = [P0, P1, P2, P3]

        x_in = [sem(f"x_in{i}") for i in range(TILES)]
        x_again = [sem(f"x_again{q}") for q in range(4)]
        ctx_in = [sem(f"ctx_in{h}") for h in range(HEADS)]
        wh_in, mask_in, wgo_in = sem("wh_in"), sem("mask_in"), sem("wgo_in")
        ww_done, ww_hi, ww_ready, w_hi, w_split = (sem("ww_done"), sem("ww_hi"), sem("ww_ready"),
                                                  sem("w_hi"), sem("w_split"))
        negated, bias_ready, xnT_hi, zT_hi, x2_ready = (sem("negated"), sem("bias_ready"), sem("xnT_hi"),
                                                        sem("zT_hi"), sem("x2_ready"))
        gb_in, wr_in, gate_in, ident_in = sem("gb_in"), sem("wr_in"), sem("gate_in"), sem("ident_in")
        pad_zero, pads_set = sem("pad_zero"), sem("pads_set")
        dve_step = sem("dve_step")
        half_set, mv_ready, var_ready, rstd_ready = (sem("half_set"), sem("mv_ready"), sem("var_ready"),
                                                    sem("rstd_ready"))
        xn_ready, xn_turned, xnT_ready = sem("xn_ready"), sem("xn_turned"), sem("xnT_ready")
        fill_done, act_evac, dve_evac = sem("fill_done"), sem("act_evac"), sem("dve_evac")
        s_done, at_ready = sem("s_done"), sem("at_ready")
        gates_ready = sem("gates_ready")
        w_done, z_ready, z_turned, zT_ready = sem("w_done"), sem("z_ready"), sem("z_turned"), sem("zT_ready")
        wo_done, xn2_ready, xn2_turned, xn2T_ready = (sem("wo_done"), sem("xn2_ready"),
                                                      sem("xn2_turned"), sem("xn2T_ready"))
        xn2_out = [sem(f"xn2_out{q}") for q in range(2)]
        xn2T_out = [sem(f"xn2T_out{q}") for q in range(2)]
        logits_done = sem("logits_done")
        block = ctx.enter_context(nc.Block())

        plan = [("V", 0, c) for c in range(4)] + [("Q", 0, c) for c in range(4)]
        for h in range(HEADS):
            plan.append(("S", h, 0))
            for kind, head in (("Q", h + 1), ("O", h), ("V", h + 1)):
                plan += [(kind, head, c) for c in range(4) if head < HEADS]
        fill_of, r = {}, 0
        for item in plan:
            if item[0] != "S":
                fill_of[item] = r
                r += 1

        TURNED_BEFORE = {("V", 0, 0): range(2, 6), ("V", 0, 1): range(6, 8), ("V", 0, 2): range(8, 10),
                         ("V", 0, 3): range(10, 12), ("Q", 0, 0): range(12, TILES)}

        slot_order = [(i, EPS1) for i in range(TILES)] + [(TILES, EPS_GN), (TILES + 1, EPS_GN)]
        for t in range(TILES + 2):
            if t + 2 < TILES:
                slot_order.append((TILES + t + 2, EPS_GN))
            if t >= 2:
                slot_order.append((2 * TILES + t - 2, EPS1))
        turn_of = {slot: n for n, (slot, _) in enumerate(slot_order)}

        def destination(kind, h, c):
            if kind == "Q":
                return QT[:, c * 512:(c + 1) * 512]
            if kind == "V":
                return V[:, :, 2 * c:2 * c + 2, :].rearrange("p t b e -> p b t e")
            return O[:, c // 2, 4 * (c % 2):4 * (c % 2) + 4, h, :]

        def source(kind, bank):
            if kind == "V":
                return bank[:, :].rearrange("p (b t e) -> p b t e", b=2, t=2)
            if kind == "O":
                return bank[:, :].rearrange("p (b e) -> p b e", b=4)
            return bank[:, :]

        @block.sync
        def _(sp):
            def load_x(i, again=False):
                if again and i < 4:
                    sp.wait_ge(xn_turned, TILES)
                elif again:
                    sp.wait_ge(x2_ready, i - 3)
                dst, done = (x[:, i % 4, :], x_again[i % 4]) if again else (x2[:, i, :], x_in[i])
                sp.dma_start(dst, io["x"][i * P:(i + 1) * P, :]).then_inc(done, 16)

            for i in range(4):
                load_x(i)
            sp.dma_start(ident[:, :], io["ident"]).then_inc(ident_in, 16)
            sp.dma_start(wh[:, :, :], io["wh"].rearrange("h d e -> d h e")).then_inc(wh_in, 16)
            sp.dma_start(whT, io["whT"]).then_inc(wh_in, 16)
            for i in range(4, TILES):
                load_x(i)
                if i == 6:
                    sp.dma_start(ctxT[:, 0, :], io["ctxT"][0:P, :]).then_inc(ctx_in[0], 16)
            sp.dma_start(mask[:, :, :, :], io["mask"]).then_inc(mask_in, 16)
            sp.dma_start(ctxT[:, 1, :], io["ctxT"][P:2 * P, :]).then_inc(ctx_in[1], 16)
            sp.wait_ge(xn_ready, 2 * KD)
            sp.dma_start(w_whole[:, 0:KD, :], io["wg"].rearrange("(k p) n -> p k n", p=P)).then_inc(wgo_in, 16)
            sp.dma_start(w_whole[:, KD:2 * KD, :], io["wo"].rearrange("(k p) n -> p k n", p=P)).then_inc(wgo_in, 16)
            sp.dma_start(wr[:, :, :], io["wrT"].rearrange("(k p) n -> p k n", p=P)).then_inc(wr_in, 16)
            sp.dma_start(gamma[:, :], io["gamma"].to_broadcast([P, D])).then_inc(gb_in, 16)
            sp.dma_start(beta[:, :], io["beta"].to_broadcast([P, D])).then_inc(gb_in, 16)
            sp.wait_ge(pad_zero, 1)
            for q in range(ROUTED // 3):
                sp.dma_start(io["slots"][3 * P * q:3 * P * (q + 1), :].rearrange("(t p) d -> p t d", p=P),
                             zeros[:, :].unsqueeze(1).to_broadcast([P, 3, D])).then_inc(pads_set, 16)
            for h in range(2, HEADS):
                sp.wait_ge(s_done, 2 * (h - 1))
                sp.dma_start(ctxT[:, h % 2, :], io["ctxT"][h * P:(h + 1) * P, :]).then_inc(ctx_in[h], 16)
            for i in range(4):
                load_x(i, again=True)
            sp.wait_ge(s_done, 2 * HEADS)
            for piece in range(PLACES):
                load_piece(io, keep, sp, 0, piece)
            for i in range(TILES):
                if i + 4 < TILES:
                    load_x(i + 4, again=True)
                sp.wait_ge(xn2_ready, i + 1)
                sp.dma_start(io["xn2"][i * P:(i + 1) * P, :], xn[:, i % 2, :]).then_inc(xn2_out[i % 2], 16)
                sp.wait_ge(xn2T_ready, i + 1)
                sp.dma_start(io["xn2T"][i], xn2T[:, i % 2, :, :]).then_inc(xn2T_out[i % 2], 16)
            sp.wait_ge(pads_set, 16 * ROUTED // 3)
            for q in range(2):
                sp.wait_ge(xn2_out[q], 16 * TILES // 2)
                sp.wait_ge(xn2T_out[q], 16 * TILES // 2)

        @block.gpsimd
        def _(pool):
            nc.gpsimd.memset(zeros[:, :], 0.0).then_inc(pad_zero, 1)
            nc.gpsimd.memset(neg_half[:, :], -0.5).then_inc(half_set, 1)
            pool.wait_ge(half_set, 1)
            for n, (slot, eps) in enumerate(slot_order):
                pool.wait_ge(mv_ready, n + 1)
                nc.gpsimd.tensor_scalar(var_eps[:, slot:slot + 1], mv[:, slot, 1:2], eps, None,
                                        ALU.add).then_inc(var_ready, 1)
                pool.wait_ge(var_ready, n + 1)
                nc.gpsimd.tensor_tensor(rstd[:, slot:slot + 1], var_eps[:, slot:slot + 1], neg_half[:, :],
                                        ALU.pow).then_inc(rstd_ready, 1)
                if n < TILES:
                    nc.gpsimd.tensor_scalar(bias[:, n, 0:1], mv[:, n, 0:1], -1.0, None, ALU.mult).then_inc(negated, 1)
                    pool.wait_ge(negated, n + 1)
                    pool.wait_ge(rstd_ready, n + 1)
                    nc.gpsimd.tensor_tensor(bias[:, n, 1:2], bias[:, n, 0:1], rstd[:, n:n + 1],
                                            ALU.mult).then_inc(bias_ready, 1)

        @block.scalar
        def _(act):
            act.dma_start(keep["gates"][:, 0:1], io["g_xattn"].to_broadcast([P, 1])).then_inc(gate_in, 16)
            act.dma_start(keep["gates"][:, 1:2], io["g_ffn"].to_broadcast([P, 1])).then_inc(gate_in, 16)
            act.wait_ge(gate_in, 32)
            nc.scalar.activation(keep["tanh"][:, :], keep["gates"][:, :], ACT.Tanh).then_inc(gates_ready, 1)
            def take_out(item):
                r = fill_of.get(item)
                if r is not None and r % 2 == 0:
                    if item == ("O", 0, 0):
                        act.wait_ge(w_split, 2 * KD)
                        act.wait_ge(xn_ready, TILES)
                    act.wait_ge(fill_done, r + 1)
                    nc.scalar.activation(destination(*item), source(item[0], ring[r % 4]),
                                         ACT.Copy).then_inc(act_evac, 1)

            for t in range(TILES + 2):
                i = t - 2
                if i >= 0:
                    act.wait_ge(xn_turned, i + 1)
                    nc.scalar.activation(xnT[0][:, :, i * P:(i + 1) * P],
                                         (T0, T1, S1)[i % 3][:, :].rearrange("p (k n) -> p k n", k=KD),
                                         ACT.Copy).then_inc(xnT_hi, 1)
                i = t
                if i < TILES:
                    act.wait_ge(bias_ready, i + 1)
                    if i >= 4:
                        act.wait_ge(xn_turned, i - 3)
                    nc.scalar.activation(x[:, i % 4, :], x2[:, i, :], ACT.Identity, bias=bias[:, i, 1:2],
                                         scale=rstd[:, i:i + 1]).then_inc(xn_ready, 1)
                if t == 4:
                    act.wait_ge(ww_done, HEADS)
                    nc.scalar.activation(wwT[0][:, :, :], S0[:, :].rearrange("p (h d) -> p h d", h=HEADS),
                                         ACT.Copy).then_inc(ww_hi, 1)
                if t in (10, 14):
                    take_out(("V", 0, (t - 10) // 2))
            for item in plan:
                if item == ("S", 0, 0):
                    act.wait_ge(wgo_in, 32)
                    for k in range(2 * KD):
                        nc.scalar.activation(wgo[0][:, k, :], w_whole[:, k, :], ACT.Copy).then_inc(w_hi, 1)
                elif item[:2] != ("V", 0):
                    take_out(item)
            for t in range(TILES + 5):
                i = t - 1
                if 0 <= i < TILES:
                    act.wait_ge(z_turned, i + 1)
                    if i >= 2:
                        act.wait_ge(wo_done, i - 1)
                    nc.scalar.activation(ZT[0][:, i % 2, :, :], (T0, T1)[i % 2][:, :].rearrange("p (k n) -> p k n", k=KD),
                                         ACT.Copy).then_inc(zT_hi, 1)
                i = t - 4
                if 0 <= i < TILES:
                    act.wait_ge(xn2_turned, i + 1)
                    if i >= 2:
                        act.wait_ge(logits_done, i - 1)
                        act.wait_ge(xn2T_out[i % 2], 16 * (i // 2))
                    nc.scalar.activation(xn2T[:, i % 2, :, :], P2[:, :].rearrange("p (k n) -> p k n", k=KD),
                                         ACT.Copy).then_inc(xn2T_ready, 1)

        @block.tensor
        def _(pe):
            pe.wait_ge(ident_in, 16)

            def turn_xn(i):
                pe.wait_ge(xn_ready, i + 1)
                if i >= 3:
                    pe.wait_ge(xnT_ready, i - 2)
                for k in range(KD):
                    last = nc.tensor.transpose((T0, T1, S1)[i % 3][:, k * P:(k + 1) * P],
                                               x[:, i % 4, k * P:(k + 1) * P], ident[:, :])
                last.then_inc(xn_turned, 1)

            turn_xn(0)
            turn_xn(1)
            pe.wait_ge(wh_in, 32)
            for h in range(HEADS):
                nc.tensor.matmul(S0[:, h * HD:(h + 1) * HD], whT[:, h, :], whT[:, h, :], start=True,
                                 stop=True).then_inc(ww_done, 1)
            for kind, h, c in plan:
                for i in TURNED_BEFORE.get((kind, h, c), ()):
                    turn_xn(i)
                if (kind, h, c) == ("Q", 0, 0):
                    pe.wait_ge(xnT_ready, TILES)
                    pe.wait_ge(ww_ready, 1)
                if kind == "S":
                    pe.wait_ge(act_evac, (fill_of[("Q", h, 3)] + 1) // 2)
                    pe.wait_ge(dve_evac, (fill_of[("Q", h, 3)] + 1) // 2)
                    if h:
                        pe.wait_ge(at_ready, 2 * h)
                    for tc in range(2):
                        for b in range(B):
                            last = nc.tensor.matmul((S0, S1)[tc][:, tc * P:S],
                                                    ctxT[:, h % 2, b * S + tc * P:b * S + tc * P + P],
                                                    QT[:, b * S + tc * P:(b + 1) * S],
                                                    start=(b == 0), stop=(b == B - 1))
                        last.then_inc(s_done, 1)
                    continue
                r = fill_of[(kind, h, c)]
                if r >= 4:
                    pe.wait_ge((act_evac, dve_evac)[r % 2], (r - 4) // 2 + 1)
                bank = ring[r % 4]
                if kind == "Q":
                    for g, (a, b) in enumerate(PARTS):
                        last = nc.tensor.matmul(bank[:, :], wwT[a][:, h, :], xnT[b][:, h, c * 512:(c + 1) * 512],
                                                start=(g == 0), stop=(g == 2))
                elif kind == "V":
                    pe.wait_ge(ctx_in[h], 16)
                    for q in range(4):
                        n0 = (4 * c + q) * P
                        last = nc.tensor.matmul(bank[:, q * P:(q + 1) * P], ctxT[:, h % 2, n0:n0 + P],
                                                wh[:, h, :], start=True, stop=True)
                else:
                    pe.wait_ge(at_ready, 2 * h + 2)
                    pe.wait_ge(act_evac, (fill_of[("V", h, 3)] + 1) // 2)
                    pe.wait_ge(dve_evac, (fill_of[("V", h, 3)] + 1) // 2)
                    sc, bg = c // 2, c % 2
                    for tc in range(2):
                        last = nc.tensor.matmul(bank[:, :], AT[:, h % 2, tc, sc * P:(sc + 1) * P],
                                                V[:, tc, 4 * bg:4 * bg + 4, :],
                                                start=(tc == 0), stop=(tc == 1))
                last.then_inc(fill_done, 1)
            pe.wait_ge(act_evac, r // 2 + 1)
            pe.wait_ge(dve_evac, r // 2 + 1)
            for t in range(TILES + 5):
                i = t
                if i < TILES:
                    if i == 0:
                        pe.wait_ge(w_split, 2 * KD)
                    if i >= 2:
                        pe.wait_ge(z_ready, i - 1)
                    for g, (a, b) in enumerate(PARTS):
                        for k in range(KD):
                            last = nc.tensor.matmul((P0, P1)[i % 2][:, :], xnT[a][:, k, i * P:(i + 1) * P],
                                                    wgo[b][:, k, :], start=(g == 0 and k == 0),
                                                    stop=(g == 2 and k == KD - 1))
                    last.then_inc(w_done, 1)
                i = t - 1
                if 0 <= i < TILES:
                    pe.wait_ge(z_ready, i + 1)
                    if i >= 2:
                        pe.wait_ge(zT_ready, i - 1)
                    for k in range(KD):
                        last = nc.tensor.transpose((T0, T1)[i % 2][:, k * P:(k + 1) * P],
                                                   Z[:, i % 2, k * P:(k + 1) * P], ident[:, :])
                    last.then_inc(z_turned, 1)
                i = t - 2
                if 0 <= i < TILES:
                    if i == 0:
                        pe.wait_ge(at_ready, 2 * HEADS)
                    pe.wait_ge(zT_ready, i + 1)
                    if i >= 2:
                        pe.wait_ge(x2_ready, i - 1)
                    for g, (a, b) in enumerate(PARTS):
                        for k in range(KD):
                            last = nc.tensor.matmul((S0, S1)[i % 2][:, :], ZT[a][:, i % 2, k, :],
                                                    wgo[b][:, KD + k, :], start=(g == 0 and k == 0),
                                                    stop=(g == 2 and k == KD - 1))
                    last.then_inc(wo_done, 1)
                i = t - 4
                if 0 <= i < TILES:
                    pe.wait_ge(xn2_ready, i + 1)
                    if i >= 1:
                        pe.wait_ge(xn2T_ready, i)
                    for k in range(KD):
                        last = nc.tensor.transpose(P2[:, k * P:(k + 1) * P], xn[:, i % 2, k * P:(k + 1) * P],
                                                   ident[:, :])
                    last.then_inc(xn2_turned, 1)
                i = t - 5
                if 0 <= i < TILES:
                    if i == 0:
                        pe.wait_ge(wr_in, 16)
                    pe.wait_ge(xn2T_ready, i + 1)
                    for k in range(KD):
                        last = nc.tensor.matmul(P3[:, i * E:(i + 1) * E], xn2T[:, i % 2, k, :], wr[:, k, :],
                                                start=(k == 0), stop=(k == KD - 1))
                    last.then_inc(logits_done, 1)

        @block.vector
        def _(dve):
            count = [0]

            def link(ins):
                count[0] += 1
                ins.then_inc(dve_step, 1)
                dve.wait_ge(dve_step, count[0])

            def moments(src, slot):
                link(nc.vector.bn_stats(stats[:, slot, :], src))
                nc.vector.bn_aggr(mv[:, slot, :], stats[:, slot, :]).then_inc(mv_ready, 1)

            def normalised(out, src, slot):
                dve.wait_ge(mv_ready, turn_of[slot] + 1)
                dve.wait_ge(rstd_ready, turn_of[slot] + 1)
                return nc.vector.tensor_scalar(out, src, mv[:, slot, 0:1], rstd[:, slot:slot + 1],
                                               ALU.subtract, ALU.mult)

            def take_out(item):
                r = fill_of[item]
                if r % 2:
                    if item == ("O", 0, 1):
                        dve.wait_ge(w_split, 2 * KD)
                        dve.wait_ge(xn_ready, TILES)
                    dve.wait_ge(fill_done, r + 1)
                    nc.vector.tensor_copy(destination(*item), source(item[0], ring[r % 4])).then_inc(dve_evac, 1)

            for t in range(TILES + 3):
                if t < TILES:
                    dve.wait_ge(x_in[t], 16)
                    moments(x2[:, t, :], t)
                i = t - 3
                if i >= 0:
                    dve.wait_ge(xnT_hi, i + 1)
                    nc.vector.tensor_tensor(xnT[1][:, :, i * P:(i + 1) * P],
                                            (T0, T1, S1)[i % 3][:, :].rearrange("p (k n) -> p k n", k=KD),
                                            xnT[0][:, :, i * P:(i + 1) * P].bitcast(F32),
                                            ALU.subtract).then_inc(xnT_ready, 1)
                if t == 5:
                    dve.wait_ge(ww_hi, 1)
                    nc.vector.tensor_tensor(wwT[1][:, :, :], S0[:, :].rearrange("p (h d) -> p h d", h=HEADS),
                                            wwT[0][:, :, :].bitcast(F32), ALU.subtract).then_inc(ww_ready, 1)
                    link(nc.vector.memset(AT[:, :, 1, 0:P], 1.0))
                if t in (12, 16):
                    take_out(("V", 0, (t - 10) // 2))
            dve.wait_ge(mask_in, 16)
            for item in plan:
                if item[0] == "S":
                    h = item[1]
                    if h == 0:
                        for k in range(2 * KD):
                            dve.wait_ge(w_hi, k + 1)
                            nc.vector.tensor_tensor(wgo[1][:, k, :], w_whole[:, k, :], wgo[0][:, k, :].bitcast(F32),
                                                    ALU.subtract).then_inc(w_split, 1)
                    for tc in range(2):
                        if h or tc:
                            dve.wait_ge(at_ready, 2 * h + tc)
                        dve.wait_ge(s_done, 2 * h + tc + 1)
                        m, at = masked[:, tc * P:S], AT[:, h % 2, tc, tc * P:S]
                        link(nc.vector.tensor_tensor(m, (S0, S1)[tc][:, tc * P:S], mask[:, h, tc, tc * P:S], ALU.mult))
                        link(nc.vector.tensor_scalar(at, m, -1.0, 1.0, ALU.mult, ALU.max))
                        nc.vector.tensor_tensor(at, at, m, ALU.max).then_inc(at_ready, 1)
                    continue
                if item[:2] != ("V", 0):
                    take_out(item)
            dve.wait_ge(act_evac, (len(fill_of) + 1) // 2)
            dve.wait_ge(dve_evac, len(fill_of) // 2)
            dve.wait_ge(gb_in, 32)
            dve.wait_ge(gates_ready, 1)

            def o_rows(i):
                return O[:, i % 2, i // 2, :, :].rearrange("p h e -> p (h e)")

            moments(o_rows(0), TILES)
            moments(o_rows(1), TILES + 1)
            for t in range(TILES + 3):
                if t + 2 < TILES:
                    moments(o_rows(t + 2), TILES + t + 2)
                i = t
                if i < TILES:
                    if i:
                        dve.wait_ge(z_ready, i)
                    link(normalised(Y, o_rows(i), TILES + i))
                    link(nc.vector.tensor_tensor(Y, Y, gamma[:, :], ALU.mult))
                    link(nc.vector.tensor_tensor(Y, Y, beta[:, :], ALU.add))
                    dve.wait_ge(w_done, i + 1)
                    if i >= 2:
                        dve.wait_ge(z_turned, i - 1)
                    nc.vector.scalar_tensor_tensor(Z[:, i % 2, :], (P0, P1)[i % 2][:, :], 0.0, Y,
                                                   ALU.max, ALU.mult).then_inc(z_ready, 1)
                i = t - 1
                if 0 <= i < TILES:
                    dve.wait_ge(zT_hi, i + 1)
                    nc.vector.tensor_tensor(ZT[1][:, i % 2, :, :], (T0, T1)[i % 2][:, :].rearrange("p (k n) -> p k n", k=KD),
                                            ZT[0][:, i % 2, :, :].bitcast(F32), ALU.subtract).then_inc(zT_ready, 1)
                i = t - 2
                if 0 <= i < TILES:
                    dve.wait_ge(wo_done, i + 1)
                    dve.wait_ge(x_again[i % 4], 16 * (i // 4 + 1))
                    nc.vector.scalar_tensor_tensor(x2[:, i, :], (S0, S1)[i % 2][:, :], keep["tanh"][:, 0:1],
                                                   x[:, i % 4, :], ALU.mult, ALU.add).then_inc(x2_ready, 1)
                    dve.wait_ge(x2_ready, i + 1)
                    moments(x2[:, i, :], 2 * TILES + i)
                i = t - 3
                if 0 <= i < TILES:
                    if i >= 2:
                        dve.wait_ge(xn2_turned, i - 1)
                        dve.wait_ge(xn2_out[i % 2], 16 * (i // 2))
                    normalised(xn[:, i % 2, :], x2[:, i, :], 2 * TILES + i).then_inc(xn2_ready, 1)

            dve.wait_ge(logits_done, TILES)
            nc.vector.tensor_copy(keep["logits"][:, :], P3[:, 0:TILES * E]).then_inc(dve_step, 1)


def route_and_feed_forward(nc, io, keep, banks):
    ctx = ExitStack()
    with ctx:
        def sb(name, shape, dt=F32):
            return ctx.enter_context(nc.sbuf_tensor(name, shape, dt))

        def sem(name):
            return ctx.enter_context(nc.semaphore(name))

        ident = keep["ident"]
        places, piece_in = keep["places"], keep["piece_in"]
        rows = places[:, RING:PLACES, :]
        w = [sb(f"w_{x}", [P, 2, WIDTH], F32R) for x in ("hi", "lo")]
        xg = sb("xg", [P, D])
        xT = [sb(f"xT_{x}", [P, KD, P], F32R) for x in ("hi", "lo")]
        hid = sb("hid", [P, HID])
        tail = sb("tail", [P, P], F32R)
        hT = [sb("hT_hi", [P, HC + 1, P], F32R), sb("hT_lo", [P, HC, P], F32R)]
        out_sb = sb("out_sb", [P, D])
        lt = sb("lt", [P, 5, TILES * E])
        tri = sb("tri", [P, 2, P])
        thr = out_sb[:, 0:ROUTED * (E - 1)]
        small = sb("small", [P, 5, TILES])
        cst = sb("cst", [P, E + E * THR + ROUTED + 1])
        lo_rows = cst[0:3 * HT, E + E * THR + ROUTED:]
        ends = sb("ends", [P, 2, E])
        expert = sb("expert", [P, ROUTED])
        gate_of = sb("gate_of", [P, 2, TILES])
        slot = sb("slot", [P, 2 * TILES], I32)
        parity = sb("parity", [P, ROUTED], I32)
        needs = sb("needs", [P, 2, ROUTED], I32)
        free_at = sb("free_at", [P, 2, E - 1], I32)

        up_bank, hturn_bank, xturn_bank, down_bank, rank_bank = banks[0:3], banks[3:5], banks[5], banks[6], banks[7]

        buffer_free = sem("buffer_free")
        zeroed, hi_other, split_other, hi_split, split = sem("zeroed"), sem("hi_other"), sem("split_other"), sem("hi_split"), sem("split")
        tail_hi, tail_ready, masked = sem("tail_hi"), sem("tail_ready"), sem("masked")
        x_in, x_turned, x_hi, x_lo = sem("x_in"), sem("x_turned"), sem("x_hi"), sem("x_lo")
        up_done, silu_done, h_done = sem("up_done"), sem("silu_done"), sem("h_done")
        h_turned, h_hi, h_lo = sem("h_turned"), sem("h_hi"), sem("h_lo")
        down_done, down_taken, out_ready, stored = sem("down_done"), sem("down_taken"), sem("out_ready"), sem("stored")
        cst_in, dve_step, shifted, exped, chosen, ranked = (sem("cst_in"), sem("dve_step"), sem("shifted"),
                                                           sem("exped"), sem("chosen"), sem("ranked"))
        slots_ready, tables_ready = sem("slots_ready"), sem("tables_ready")
        tile_in = [sem(f"tile_in{q}") for q in range(4)]
        tile_out = [sem(f"tile_out{q}") for q in range(4)]
        row_in = [sem(f"row_in{q}") for q in range(4)]
        row_added, y_out = sem("row_added"), sem("y_out")
        block = ctx.enter_context(nc.Block())

        shared_tile = list(range(FIRST)) + [None] * ROUTED + list(range(FIRST, TILES))

        def comes_turned(s):
            return isinstance(s, int) and shared_tile[s] is not None

        def x_source(s):
            return xg[:, :] if comes_turned(s) else xturn_bank[:, :]

        def pair(i):
            return places[:, 2 * (i % 4):2 * (i % 4) + 2, :]

        def part(q, buf, piece):
            c0, n, rows_ = PIECES[piece]
            if piece == NP - 1:
                q = 1 - q
            return w[q][0:rows_, buf, c0:c0 + n]

        def added_in(m):
            n = -(-TILES // (LAST - 2))
            return range(n * (m - 2), min(n * (m - 1), TILES)) if 2 <= m < LAST else range(0)

        def complete_at(i):
            return max(i - FIRST + 1, next(m for m in range(1, LAST + 1) if i in added_in(m)))

        @block.sync
        def _(sp):
            def load(version, piece):
                n = version * NP + piece
                m = before(n)
                if m < NP:
                    sp.wait_ge(split_other, m + 1)
                elif m < NP + POOL_FIRST:
                    sp.wait_ge(split, m - NP + 1)
                elif m < 2 * NP:
                    sp.wait_ge(split_other, m + 1 - POOL_FIRST)
                else:
                    sp.wait_ge(split, m - NP - OTHERS + 1)
                load_piece(io, keep, sp, version, piece)

            def load_tile(i):
                if i < 4:
                    sp.wait_ge(split_other, PLACES)
                else:
                    sp.wait_ge(tile_out[i % 4], 32 * (i // 4))
                sp.dma_start(rows[:, i % 4, :], io["xn2"][i * P:(i + 1) * P, :]).then_inc(tile_in[i % 4], 16)

            sp.dma_start(xg[:, :], io["xn2T"][0].rearrange("p k n -> p (k n)")).then_inc(x_in, 16)
            sp.dma_start(tri[:, :, :], io["tri"]).then_inc(cst_in, 16)
            sp.dma_start(cst[:, :], io["cst"]).then_inc(cst_in, 16)
            for piece in range(PLACES, NP):
                load(0, piece)
            for i in range(4):
                load_tile(i)
            for piece in range(POOL_FIRST):
                load(1, piece)
            for i in range(4, TILES):
                load_tile(i)
                if POOL_FIRST + i - 4 < NP:
                    load(1, POOL_FIRST + i - 4)
            for version in range(2, len(ORDER)):
                for piece in range(NP):
                    load(version, piece)

        @block.gpsimd
        def _(pool):
            def split_pieces(version, first, end):
                for piece in range(first, end + 1):
                    if piece < end:
                        n = version * NP + piece
                        c0, cols, rows_ = PIECES[piece]
                        q, nth = place(n)
                        pool.wait_ge(piece_in[q], 16 * nth)
                        nc.gpsimd.tensor_copy(part(0, version % 2, piece),
                                              places[0:rows_, place(n)[0], 0:cols]).then_inc(hi_split, 1)
                    if piece > first:
                        n = version * NP + piece - 1
                        c0, cols, rows_ = PIECES[piece - 1]
                        pool.wait_ge(hi_split, n + 1 - NP - (OTHERS if version > 1 else 0))
                        if piece == NP:
                            nc.gpsimd.tensor_scalar(places[0:rows_, place(n)[0], 0:cols], places[0:rows_, place(n)[0], 0:cols],
                                                    lo_rows, None, ALU.mult).then_inc(masked, 1)
                            pool.wait_ge(masked, version - 1)
                        nc.gpsimd.tensor_tensor(part(1, version % 2, piece - 1), places[0:rows_, place(n)[0], 0:cols],
                                                part(0, version % 2, piece - 1).bitcast(F32),
                                                ALU.subtract).then_inc(split, 1)

            pool.wait_ge(cst_in, 32)
            split_pieces(1, 0, POOL_FIRST)
            pool.wait_ge(slots_ready, 2)
            for i in range(TILES):
                pool.wait_ge(tile_in[i % 4], 16 * (i // 4 + 1))
                for c in range(2):
                    nc.gpsimd.indirect_dma_start(
                        out=io["slots"], out_offset=bass.IndirectOffsetOnAxis(slot[:, c * TILES + i:c * TILES + i + 1], 0),
                        in_=rows[:, i % 4, :], in_offset=None).then_inc(tile_out[i % 4], 16)
            pool.wait_ge(up_done, 3 * FIRST)
            split_pieces(2, 0, NU)
            pool.wait_ge(down_done, FIRST)
            split_pieces(2, NU, NP)
            pool.wait_ge(tables_ready, 3)
            for version in range(3, len(ORDER)):
                for q, (done, lowest, first, end) in enumerate(((up_done, 3, 0, NU), (down_done, 1, NU, NP))):
                    at = pool.value_load(free_at[0:1, q, version - 3:version - 2], min_val=lowest * (FIRST + 1),
                                         max_val=lowest * (FIRST + ROUTED))
                    pool.wait_ge(done, at)
                    pool.sem_inc(buffer_free, 1)
                    pool.wait_ge(buffer_free, 2 * (version - 3) + q + 1)
                    split_pieces(version, first, end)
            for q in range(4):
                pool.wait_ge(tile_out[q], 32 * TILES // 4)
            pool.wait_ge(split, NP * (len(ORDER) - 1) - OTHERS)
            pool.wait_ge(stored, 16 * ROUTED)
            for i in range(TILES):
                if i >= 4:
                    pool.wait_ge(row_added, 2 * (i - 3))
                for c in range(2):
                    nc.gpsimd.indirect_dma_start(
                        out=pair(i)[:, c, :], out_offset=None, in_=io["routed"],
                        in_offset=bass.IndirectOffsetOnAxis(slot[:, c * TILES + i:c * TILES + i + 1], 0)
                    ).then_inc(row_in[i % 4], 16)

        @block.scalar
        def _(act):
            def load_x(s, loop=None):
                if loop is not None:
                    act.dma_start(xg[:, :], io["slots"][bass.ds(loop * P, P), :]).then_inc(x_in, 16)
                    return
                if s >= STEPS:
                    return
                if s == FIRST:
                    for q in range(4):
                        act.wait_ge(tile_out[q], 32 * TILES // 4)
                i = shared_tile[s]
                if s and shared_tile[s - 1] is not None:
                    act.wait_ge(x_lo, s)
                src = io["slots"][(s - FIRST) * P:(s - FIRST + 1) * P, :] if i is None else \
                    io["xn2T"][i].rearrange("p k n -> p (k n)")
                act.dma_start(xg[:, :], src).then_inc(x_in, 16)

            def high(version, piece):
                n = version * NP + piece
                c0, cols, rows_ = PIECES[piece]
                q, nth = place(n)
                act.wait_ge(piece_in[q], 16 * nth)
                nc.scalar.activation(part(0, version, piece), places[0:rows_, place(n)[0], 0:cols], ACT.Copy).then_inc(hi_other, 1)

            def tail_high(s):
                act.wait_ge(h_done, 3 * s + 3)
                nc.scalar.activation(tail[:, HT:2 * HT], hid[:, HC * P:HID], ACT.Copy).then_inc(tail_hi, 1)
                nc.scalar.activation(tail[:, 2 * HT:3 * HT], hid[:, HC * P:HID], ACT.Copy,
                                     scale=-1.0).then_inc(tail_hi, 1)

            def x_high(s):
                if comes_turned(s):
                    act.wait_ge(x_in, 16 * (s + 1))
                else:
                    act.wait_ge(x_turned, s - FIRST + 1)
                nc.scalar.activation(xT[0][:, :, :], x_source(s).rearrange("p (k n) -> p k n", k=KD),
                                     ACT.Copy).then_inc(x_hi, 1)

            def h_high(s):
                for q, (a, b) in enumerate(((0, 4), (4, 6))):
                    act.wait_ge(h_turned, 2 * s + q + 1)
                    nc.scalar.activation(hT[0][:, a:b, :], hturn_bank[q][:, 0:(b - a) * P].rearrange("p (k n) -> p k n", k=b - a),
                                         ACT.Copy).then_inc(h_hi, 1)

            def iteration(s, up=True, turn=True, down=True, routed_down=False, loop=None):
                for c in range(3):
                    if up:
                        if c == 0 and down:
                            act.wait_ge(h_turned, 2 * s)
                        silu(s, c)
                    if c == 0 and down:
                        h_high(s - 1)
                if up:
                    tail_high(s)
                if turn:
                    x_high(s + 1)
                    load_x(s + 2, None if loop is None else loop + 2)
                if down and routed_down:
                    act.wait_ge(down_done, s)
                    m = s - FIRST
                    if loop is not None or m > 1:
                        act.wait_ge(stored, 16 * (m - 1))
                    nc.scalar.activation(out_sb[:, :], down_bank[:, :], ACT.Copy).then_inc(out_ready, 1)
                    act.wait_ge(out_ready, m + 1)
                    dst = io["routed"][(m - 1) * P:m * P, :] if loop is None else io["routed"][bass.ds((loop - 1) * P, P), :]
                    act.dma_start(dst, out_sb[:, :]).then_inc(stored, 16)

            def store_tiles(m):
                for i in range(TILES):
                    if complete_at(i) == m:
                        act.wait_ge(down_taken, FIRST + m)
                        act.wait_ge(row_added, 2 * i + 2)
                        act.dma_start(io["out"][i * P:(i + 1) * P, :], keep["x"][:, i, :]).then_inc(y_out, 16)

            def silu(s, c):
                h0, n = UP_SPANS[c]
                act.wait_ge(up_done, 3 * s + c + 1)
                nc.scalar.activation(hid[:, h0:h0 + n], up_bank[c][:, 0:n], ACT.Silu).then_inc(silu_done, 1)

            for piece in range(NP):
                high(0, piece)
                if piece + 1 == UP_NEEDS[0]:
                    x_high(0)
                if piece + 1 == UP_NEEDS[1]:
                    load_x(1)
                if piece + 1 == NU:
                    act.wait_ge(shifted, 1)
                    nc.scalar.activation(lt[:, 1, :], lt[:, 0, :], ACT.Exp).then_inc(exped, 1)
                if piece + 1 in FIRST_UPS:
                    silu(0, FIRST_UPS.index(piece + 1))
                if piece + 1 == FIRST_UPS[2]:
                    tail_high(0)
                    x_high(1)
                    load_x(2)
            for s in range(1, FIRST + 2):
                if s == FIRST + 1:
                    act.wait_ge(down_taken, FIRST)
                    act.wait_ge(tables_ready, 3)
                    act.sem_inc(out_ready, 1)
                iteration(s, routed_down=s > FIRST)
                for piece in TURNS.get(s, ()):
                    high(1, piece)
            with act.Fori(2, ROUTED - 2) as r:
                iteration(r + FIRST, routed_down=True, loop=r)
            for s in range(FIRST + ROUTED - 2, STEPS + 1):
                iteration(s, up=s < STEPS, turn=s + 1 < STEPS, routed_down=s <= FIRST + ROUTED)
                store_tiles(s - FIRST - ROUTED - 1)
            store_tiles(LAST)
            act.wait_ge(y_out, 16 * TILES)

        @block.tensor
        def _(pe):
            def turn_x(s):
                if comes_turned(s):
                    return
                pe.wait_ge(x_in, 16 * (s + 1))
                if not isinstance(s, int) or s:
                    pe.wait_ge(x_lo, s)
                for k in range(KD):
                    mm = nc.tensor.transpose(xturn_bank[:, k * P:(k + 1) * P], xg[:, k * P:(k + 1) * P], ident[:, :])
                mm.then_inc(x_turned, 1)

            def moving(q, buf, c0, n, rows_=P):
                if isinstance(buf, int):
                    return w[q][0:rows_, buf, c0:c0 + n]
                return w[q][0:rows_, bass.ds(buf, 1), c0:c0 + n].rearrange("p o n -> p (o n)")

            def up(s, c, buf):
                c0 = KD * 2 * UP_SPANS[c][0]
                n = 2 * UP_SPANS[c][1]
                if not isinstance(s, int) or s:
                    pe.wait_ge(h_done, 3 * s + c - 2)
                for g, (a, b) in enumerate(PARTS):
                    for k in range(KD):
                        mm = nc.tensor.matmul(up_bank[c][:, 0:n], xT[a][:, k, :], moving(b, buf, c0 + k * n, n),
                                              start=(g == 0 and k == 0), stop=(g == 2 and k == KD - 1))
                mm.then_inc(up_done, 1)

            def turn_h(s):
                pe.wait_ge(h_done, 3 * s + 3)
                pe.wait_ge(tail_ready, s + 1)
                if not isinstance(s, int) or s:
                    pe.wait_ge(h_lo, 2 * s)
                for j in range(HC + 1):
                    src = hid[:, j * P:(j + 1) * P] if j < HC else tail[:, :].bitcast(F32)
                    mm = nc.tensor.transpose(hturn_bank[j // 4][:, (j % 4) * P:(j % 4 + 1) * P], src, ident[:, :])
                    if j in (3, HC):
                        mm.then_inc(h_turned, 1)

            def down(s, buf, taken, n_taken):
                pe.wait_ge(h_lo, 2 * s + 2)
                if taken is not None:
                    pe.wait_ge(taken, n_taken)
                for j in range(HC):
                    for g, (a, b) in enumerate(PARTS):
                        nc.tensor.matmul(down_bank[:, :], hT[a][:, j, :], moving(b, buf, DOWN_AT + j * D, D),
                                         start=(j == 0 and g == 0), stop=False)
                mm = nc.tensor.matmul(down_bank[:, :], hT[0][0:3 * HT, HC, :],
                                      moving(0, buf, DOWN_AT + HC * D, D, 3 * HT), start=False, stop=True)
                mm.then_inc(down_done, 1)

            for s in range(FIRST + 1):
                pe.wait_ge(x_lo, s + 1)
                if s == FIRST:
                    pe.wait_ge(split, POOL_FIRST)
                    pe.wait_ge(split_other, NP + NU - POOL_FIRST)
                buf = s // FIRST
                for c in range(3):
                    if s == 0:
                        pe.wait_ge(split_other, UP_NEEDS[c])
                    up(s, c, buf)
                    if s and c == 0:
                        turn_h(s - 1)
                if s == 1:
                    pe.wait_ge(split_other, NP)
                    pe.wait_ge(cst_in, 32)
                    pe.wait_ge(chosen, 1)
                    nc.tensor.matmul(rank_bank[:, 0:TILES * E], tri[:, 0, :], lt[:, 4, :], start=True, stop=True)
                    nc.tensor.matmul(rank_bank[:, TILES * E:2 * TILES * E], tri[:, 1, :], lt[:, 4, :], start=True,
                                     stop=True).then_inc(ranked, 1)
                turn_x(s + 1)
                if s:
                    down(s - 1, 0, down_taken if s > 1 else None, s - 1)
            pe.wait_ge(split_other, NP + OTHERS)
            pe.wait_ge(tables_ready, 3)
            with pe.Fori(1, ROUTED - 1) as r:
                buf = pe.value_load(parity[0:1, bass.ds(r, 1)], min_val=0, max_val=1)
                buf_before = pe.value_load(parity[0:1, bass.ds(r - 1, 1)], min_val=0, max_val=1)
                need_up = pe.value_load(needs[0:1, 0, bass.ds(r, 1)], min_val=NU - OTHERS, max_val=NP * E)
                need_down = pe.value_load(needs[0:1, 1, bass.ds(r - 1, 1)], min_val=NP - OTHERS, max_val=NP * E)
                s = r + FIRST
                pe.wait_ge(split, need_up)
                pe.wait_ge(x_lo, s + 1)
                up(s, 0, buf)
                turn_h(s - 1)
                up(s, 1, buf)
                up(s, 2, buf)
                turn_x(s + 1)
                pe.wait_ge(split, need_down)
                down(s - 1, buf_before, out_ready, r)
            for s in range(FIRST + ROUTED - 1, STEPS + 1):
                m = s - FIRST - ROUTED
                if s < STEPS:
                    pe.wait_ge(x_lo, s + 1)
                    buf = 0 if m < 0 else 1
                    pe.wait_ge(split, NP * (E - 1 + (m >= 0)) + NU - OTHERS)
                    up(s, 0, buf)
                turn_h(s - 1)
                if s < STEPS:
                    up(s, 1, buf)
                    up(s, 2, buf)
                if s + 1 < STEPS:
                    turn_x(s + 1)
                if m == -1:
                    before = pe.value_load(parity[0:1, ROUTED - 2:ROUTED - 1], min_val=0, max_val=1)
                    need_down = pe.value_load(needs[0:1, 1, ROUTED - 2:ROUTED - 1], min_val=NP - OTHERS, max_val=NP * E)
                    pe.wait_ge(split, need_down)
                    down(s - 1, before, out_ready, s - FIRST)
                elif m <= 1:
                    pe.wait_ge(split, NP * (E + m) - OTHERS)
                    down(s - 1, m, out_ready, s - FIRST)
                else:
                    down(s - 1, 1, down_taken, FIRST + m - 1)

        @block.vector
        def _(dve):
            count = [0]

            def link(ins):
                count[0] += 1
                ins.then_inc(dve_step, 1)
                dve.wait_ge(dve_step, count[0])

            nc.vector.memset(tail[:, 3 * HT:P].bitcast(F32), 0.0).then_inc(zeroed, 1)
            dve.wait_ge(zeroed, 1)

            def low(version, piece):
                n = version * NP + piece
                c0, cols, rows_ = PIECES[piece]
                k = n if version == 0 else n - POOL_FIRST
                dve.wait_ge(hi_other, k + 1)
                whole, high = places[0:rows_, place(n)[0], 0:cols], part(0, version, piece).bitcast(F32)
                if piece < NP - 1:
                    nc.vector.tensor_tensor(part(1, version, piece), whole, high, ALU.subtract).then_inc(split_other, 1)
                else:
                    dve.wait_ge(cst_in, 32)
                    nc.vector.scalar_tensor_tensor(part(1, version, piece), whole, lo_rows, high, ALU.mult,
                                                   ALU.subtract).then_inc(split_other, 1)

            def mult(s, c):
                h0, n = UP_SPANS[c]
                dve.wait_ge(silu_done, 3 * s + c + 1)
                u = hid[:, h0:h0 + n]
                nc.vector.tensor_tensor(u, u, up_bank[c][:, n:2 * n], ALU.mult).then_inc(h_done, 1)

            def tail_low(s):
                dve.wait_ge(tail_hi, 2 * s + 2)
                nc.vector.tensor_tensor(tail[:, 0:HT], tail[:, HT:2 * HT].bitcast(F32), hid[:, HC * P:HID],
                                        ALU.subtract).then_inc(tail_ready, 1)

            def x_low(s):
                dve.wait_ge(x_hi, s + 1)
                nc.vector.tensor_tensor(xT[1][:, :, :], x_source(s).rearrange("p (k n) -> p k n", k=KD),
                                        xT[0][:, :, :].bitcast(F32), ALU.subtract).then_inc(x_lo, 1)

            def iteration(s, up=True, turn=True, down=True, add_shared=None):
                for c in range(3):
                    if up:
                        mult(s, c)
                    if c == 0 and down:
                        for q, (a, b) in enumerate(((0, 4), (4, 6))):
                            dve.wait_ge(h_hi, 2 * (s - 1) + q + 1)
                            b = min(b, HC)
                            nc.vector.tensor_tensor(hT[1][:, a:b, :],
                                                    hturn_bank[q][:, 0:(b - a) * P].rearrange("p (k n) -> p k n", k=b - a),
                                                    hT[0][:, a:b, :].bitcast(F32), ALU.subtract).then_inc(h_lo, 1)
                if up:
                    tail_low(s)
                if turn:
                    x_low(s + 1)
                if add_shared is not None:
                    i = add_shared
                    dve.wait_ge(down_done, s)
                    nc.vector.scalar_tensor_tensor(keep["x"][:, i, :], down_bank[:, :], keep["tanh"][:, 1:2],
                                                   keep["x"][:, i, :], ALU.mult, ALU.add).then_inc(down_taken, 1)

            def by_expert(n):
                return lt[:, n, :].rearrange("p (t e) -> p t e", e=E)

            def over(ap):
                return ap.unsqueeze(2).to_broadcast([P, TILES, E])

            logits = keep["logits"][:, :].rearrange("p (t e) -> p t e", e=E)
            experts = cst[:, 0:E].unsqueeze(1).to_broadcast([P, TILES, E])

            def softmax_shift():
                link(nc.vector.tensor_reduce(small[:, 0, :], logits, X, ALU.max))
                nc.vector.tensor_tensor(by_expert(0), logits, over(small[:, 0, :]), ALU.subtract).then_inc(shifted, 1)

            def choose():
                dve.wait_ge(exped, 1)
                link(nc.vector.tensor_reduce(small[:, 1, :], by_expert(1), X, ALU.add))
                link(nc.vector.reciprocal(small[:, 1, :], small[:, 1, :]))
                link(nc.vector.tensor_tensor(by_expert(1), by_expert(1), over(small[:, 1, :]), ALU.mult))
                dve.wait_ge(cst_in, 32)
                for c in range(2):
                    onehot = by_expert(2 + c)
                    link(nc.vector.tensor_reduce(small[:, 2 + c, :], by_expert(1), X, ALU.max))
                    link(nc.vector.tensor_tensor(by_expert(0), by_expert(1), over(small[:, 2 + c, :]), ALU.is_equal))
                    link(nc.vector.tensor_tensor(by_expert(0), by_expert(0), experts, ALU.mult))
                    link(nc.vector.tensor_reduce(small[:, 4, :], by_expert(0), X, ALU.min))
                    link(nc.vector.tensor_tensor(onehot, over(small[:, 4, :]), experts, ALU.is_equal))
                    if c == 0:
                        link(nc.vector.scalar_tensor_tensor(lt[:, 1, :], lt[:, 2, :], -2.0, lt[:, 1, :], ALU.mult, ALU.add))
                nc.vector.tensor_tensor(lt[:, 4, :], lt[:, 2, :], lt[:, 3, :], ALU.add).then_inc(chosen, 1)

            def weigh():
                link(nc.vector.tensor_tensor(small[:, 4, :], small[:, 2, :], small[:, 3, :], ALU.add))
                link(nc.vector.reciprocal(small[:, 4, :], small[:, 4, :]))
                link(nc.vector.tensor_scalar(small[:, 4, :], small[:, 4, :], keep["tanh"][:, 1:2], None, ALU.mult))
                for c in range(2):
                    link(nc.vector.tensor_tensor(gate_of[:, c, :], small[:, 2 + c, :], small[:, 4, :], ALU.mult))

            def find_slots():
                dve.wait_ge(ranked, 1)
                rank, total = rank_bank[:, 0:TILES * E], rank_bank[:, TILES * E:2 * TILES * E]
                link(nc.vector.tensor_copy(lt[:, 0, :], total))
                a, b, d = 0, 1, 1
                while d < TILES:
                    link(nc.vector.tensor_copy(lt[:, b, 0:d * E], lt[:, a, 0:d * E]))
                    link(nc.vector.tensor_tensor(lt[:, b, d * E:], lt[:, a, d * E:], lt[:, a, 0:(TILES - d) * E], ALU.add))
                    a, b, d = b, a, 2 * d
                counts = lt[:, a, (TILES - 1) * E:TILES * E]
                over_thr = thr[:, 0:E * THR].rearrange("p (e k) -> p e k", k=THR)
                link(nc.vector.tensor_tensor(over_thr, counts.unsqueeze(2).to_broadcast([P, E, THR]),
                                             cst[:, E:E + E * THR].rearrange("p (e k) -> p e k", k=THR), ALU.is_gt))
                link(nc.vector.tensor_reduce(ends[:, 0, :], over_thr, X, ALU.add))
                u, v, d = 0, 1, 1
                while d < E:
                    link(nc.vector.tensor_copy(ends[:, v, 0:d], ends[:, u, 0:d]))
                    link(nc.vector.tensor_tensor(ends[:, v, d:E], ends[:, u, d:E], ends[:, u, 0:E - d], ALU.add))
                    u, v, d = v, u, 2 * d
                link(nc.vector.tensor_tensor(lt[:, 4, :], lt[:, a, :], total, ALU.subtract))
                link(nc.vector.tensor_tensor(lt[:, 4, :], lt[:, 4, :], rank, ALU.add))
                link(nc.vector.memset(ends[:, v, 0:1], 0.0))
                link(nc.vector.tensor_scalar(ends[:, v, 1:E], ends[:, u, 0:E - 1], float(P), None, ALU.mult))
                link(nc.vector.tensor_tensor(by_expert(4), by_expert(4),
                                             ends[:, v, :].unsqueeze(1).to_broadcast([P, TILES, E]), ALU.add))
                for c in range(2):
                    link(nc.vector.tensor_tensor(lt[:, 0, :], lt[:, 2 + c, :], lt[:, 4, :], ALU.mult))
                    link(nc.vector.tensor_reduce(small[:, c, :], by_expert(0), X, ALU.add))
                    nc.vector.tensor_copy(slot[:, c * TILES:(c + 1) * TILES], small[:, c, :]).then_inc(slots_ready, 1)
                return ends[:, u, 0:E - 1]

            def tables(end):
                at = thr.rearrange("p (s e) -> p s e", e=E - 1)
                link(nc.vector.tensor_tensor(at, end.unsqueeze(1).to_broadcast([P, ROUTED, E - 1]),
                                             cst[:, E + E * THR:E + E * THR + ROUTED].unsqueeze(2).to_broadcast([P, ROUTED, E - 1]), ALU.is_le))
                link(nc.vector.tensor_reduce(expert[:, :], at, X, ALU.add))
                for q, n in enumerate((NU, NP)):
                    link(nc.vector.tensor_scalar(needs[:, q, :], expert[:, :], float(NP), float(n - OTHERS), ALU.mult, ALU.add))
                link(nc.vector.tensor_scalar(expert[:, :], expert[:, :], 1.0, None, ALU.add))
                link(nc.vector.tensor_copy(parity[:, :], expert[:, :]))
                nc.vector.tensor_scalar(parity[:, :], parity[:, :], 1, None, ALU.bitwise_and).then_inc(tables_ready, 1)
                for q, n in enumerate((3.0, 1.0)):
                    nc.vector.tensor_scalar(free_at[:, q, :], end, n, n * FIRST, ALU.mult, ALU.add).then_inc(tables_ready, 1)

            for piece in range(NP):
                low(0, piece)
                if piece + 1 == UP_NEEDS[0]:
                    x_low(0)
                    softmax_shift()
                if piece + 1 in FIRST_UPS:
                    mult(0, FIRST_UPS.index(piece + 1))
                if piece + 1 == FIRST_UPS[2]:
                    tail_low(0)
                    x_low(1)
            choose()
            weigh()
            for s in range(1, FIRST + 1):
                if s == 2:
                    end = find_slots()
                if s == 3:
                    tables(end)
                iteration(s, add_shared=shared_tile[s - 1])
                for piece in TURNS.get(s, ()):
                    low(1, piece)
            with dve.Fori(1, ROUTED - 1) as r:
                iteration(r + FIRST)
            for s in range(FIRST + ROUTED - 1, STEPS + 1):
                m = s - FIRST - ROUTED
                iteration(s, up=s < STEPS, turn=s + 1 < STEPS)
                if m < 1:
                    continue
                dve.wait_ge(down_taken, FIRST + m - 1)
                for i in added_in(m):
                    dve.wait_ge(row_in[i % 4], 32 * (i // 4 + 1))
                    for c in range(2):
                        nc.vector.scalar_tensor_tensor(keep["x"][:, i, :], pair(i)[:, c, :],
                                                       gate_of[:, c, i:i + 1], keep["x"][:, i, :],
                                                       ALU.mult, ALU.add).then_inc(row_added, 1)
                        dve.wait_ge(row_added, 2 * i + c + 1)
                i = shared_tile[s - 1]
                dve.wait_ge(down_done, s)
                nc.vector.scalar_tensor_tensor(keep["x"][:, i, :], down_bank[:, :], keep["tanh"][:, 1:2],
                                               keep["x"][:, i, :], ALU.mult, ALU.add).then_inc(down_taken, 1)


def build(nc, io):
    io["xn2"] = nc.dram_tensor("xn2_rows", (N, D), F32, kind="Internal").ap()
    io["xn2T"] = nc.dram_tensor("xn2_turned", (TILES, P, KD, P), F32, kind="Internal").ap()
    io["slots"] = nc.dram_tensor("slot_rows", (ROUTED * P, D), F32, kind="Internal").ap()
    io["routed"] = nc.dram_tensor("routed_rows", (ROUTED * P, D), F32, kind="Internal").ap()
    with ExitStack() as ctx:
        def sb(name, shape, dt=F32):
            return ctx.enter_context(nc.sbuf_tensor(name, shape, dt))

        keep = {
            "x": sb("x_all", [P, TILES, D]),
            "ident": sb("ident", [P, P]),
            "gates": sb("gates", [P, 2]),
            "tanh": sb("tanh_gates", [P, 2]),
            "logits": sb("logits", [P, TILES * E]),
            "places": sb("places", [P, PLACES, D]),
            "piece_in": [ctx.enter_context(nc.semaphore(f"piece_in{q}")) for q in range(PLACES)],
        }
        banks = [ctx.enter_context(nc.psum_tensor(f"bank{i}", [P, 512], F32)) for i in range(8)]
        attention(nc, io, keep, banks)
        route_and_feed_forward(nc, io, keep, banks)


def decay_masks():
    gam = 1.0 - 2.0 ** (-5.0 - np.arange(HEADS, dtype=np.float64))
    idx = np.arange(S, dtype=np.float64)
    expo = idx[None, :] - idx[:, None]
    d = np.where(expo[None] <= 0, gam[:, None, None] ** np.minimum(expo, 0)[None], 0.0)
    d = d / np.sqrt(d.sum(-1))[:, None, :] / np.sqrt(float(HD))
    return d.transpose(2, 0, 1).reshape(2, P, HEADS, S).transpose(1, 2, 0, 3).astype(np.float32)


def kernel(**inputs):
    import numpy as _np
    import concourse.bacc as _bacc
    from concourse.bass_utils import run_bass_kernel_spmd as _run

    a = {k: _np.asarray(v) for k, v in inputs.items()}
    w1 = _np.concatenate([a["L0_ffn_ew1"], a["L0_ffn_sw1"][None]]).transpose(0, 2, 1)
    w3 = _np.concatenate([a["L0_ffn_ew3"], a["L0_ffn_sw3"][None]]).transpose(0, 2, 1)
    w2 = _np.concatenate([a["L0_ffn_ew2"], a["L0_ffn_sw2"][None]]).transpose(0, 2, 1)
    parts = [_np.concatenate([w1[..., h0:h0 + n], w3[..., h0:h0 + n]], axis=-1).reshape(E + 1, KD, P, 2 * n)
             .transpose(0, 2, 1, 3).reshape(E + 1, P, KD * 2 * n) for h0, n in UP_SPANS]
    cut = HC * P
    limits = _np.arange(THR) * float(P)
    limits[0] = -1.0
    cst = _np.concatenate([_np.arange(E) - 8.0, _np.tile(limits, E),
                           _np.arange(ROUTED, dtype=_np.float64), _np.zeros(1)]).astype(_np.float32)
    cst = _np.tile(cst, (P, 1))
    cst[HT:2 * HT, -1] = 1.0
    arrays = {
        "x": a["x"].reshape(N, D),
        "ctxT": a["ctx_2048"].reshape(N, D).T,
        "wh": a["L0_xattn_Wh"], "whT": a["L0_xattn_Wh"].transpose(2, 0, 1), "wg": a["L0_xattn_wg_w"], "wo": a["L0_xattn_wo_w"],
        "gamma": a["L0_xattn_gn_gamma"].reshape(1, D), "beta": a["L0_xattn_gn_beta"].reshape(1, D),
        "wrT": a["L0_ffn_wr"].T,
        "g_xattn": a["g_xattn"].reshape(1, 1), "g_ffn": a["g_ffn"].reshape(1, 1),
        "w_up": _np.concatenate(parts, axis=-1),
        "w_down": w2[:, :cut].reshape(E + 1, HC, P, D).transpose(0, 2, 1, 3),
        "w_downt": _np.concatenate([w2[:, cut:]] * 3, axis=1),
        "ident": _np.eye(P, dtype=_np.float32),
        "tri": _np.stack([_np.triu(_np.ones((P, P)), 1), _np.ones((P, P))], axis=1).astype(_np.float32),
        "mask": decay_masks(),
        "cst": cst,
    }
    nc = _bacc.Bacc("TRN2", target_bir_lowering=False, num_devices=1)
    feed, io = {}, {}
    for name, v in arrays.items():
        v = _np.ascontiguousarray(v)
        feed[f"in_{name}"] = v
        io[name] = nc.dram_tensor(f"in_{name}", v.shape, mybir.dt.from_np(v.dtype), kind="ExternalInput").ap()
    io["out"] = nc.dram_tensor("out_y", (N, D), F32, kind="ExternalOutput").ap()
    build(nc, io)
    r = _run(nc, [feed], core_ids=[0])
    return r.results[0]["out_y"].reshape(B, S, D)
```
